# Optimizing a Trainium2 kernel written in Bass

```python
import numpy as np
import jax
import jax.numpy as jnp

def _softmax(x, axis=-1):
    return jax.nn.softmax(x, axis=axis)

def _gelu(x):
    return jax.nn.gelu(x, approximate=True)

def _silu(x):
    return jax.nn.silu(x)

def _sigmoid(x):
    return jax.nn.sigmoid(x)

def _layernorm(x, axis=-1, eps=1e-05):
    m = jnp.mean(x, axis=axis, keepdims=True)
    v = jnp.var(x, axis=axis, keepdims=True)
    return (x - m) / jnp.sqrt(v + eps)

def _scatter_add(tgt, idx, src, axis=0):
    return tgt.at[idx].add(src)

def _segment_sum(src, seg, n):
    return jax.ops.segment_sum(src, seg, n)
kernel_name = 'mk_dlrm_tower_d1_rec_r8_5ebdfb'

def setup_inputs(seed: int=0):
    np.random.seed(seed)
    _w = jnp.asarray

    def _rec_inputs():
        import jax
        import jax.numpy as jnp
        _tk = jax.random.key(seed)
        dense_ctx = jax.random.normal(jax.random.fold_in(_tk, 190), (2048, 16), jnp.float32)
        ids = jnp.stack([jax.random.randint(jax.random.fold_in(_tk, 200 + f), (2048,), 0, v, jnp.int32) for f, v in enumerate([125000, 125000, 125000, 125000, 1250, 125000, 1250, 1000, 1000, 12500, 125000, 12500, 1000, 1250, 1000, 125000, 1000, 1250, 12500, 1250, 1250, 125000, 12500, 1000, 125000, 125000, 12500, 1250, 1250, 1000, 125000, 1000, 1250, 125000, 1000, 1000, 1250, 125000, 1250])], axis=1)
        tbl_0 = 0.05 * jax.random.normal(jax.random.fold_in(_tk, 500 + 0), (125000, 16), jnp.float32)
        tbl_1 = 0.05 * jax.random.normal(jax.random.fold_in(_tk, 500 + 1), (125000, 16), jnp.float32)
        tbl_2 = 0.05 * jax.random.normal(jax.random.fold_in(_tk, 500 + 2), (125000, 16), jnp.float32)
        tbl_3 = 0.05 * jax.random.normal(jax.random.fold_in(_tk, 500 + 3), (125000, 16), jnp.float32)
        tbl_4 = 0.05 * jax.random.normal(jax.random.fold_in(_tk, 500 + 4), (1250, 16), jnp.float32)
        tbl_5 = 0.05 * jax.random.normal(jax.random.fold_in(_tk, 500 + 5), (125000, 16), jnp.float32)
        tbl_6 = 0.05 * jax.random.normal(jax.random.fold_in(_tk, 500 + 6), (1250, 16), jnp.float32)
        tbl_7 = 0.05 * jax.random.normal(jax.random.fold_in(_tk, 500 + 7), (1000, 16), jnp.float32)
        tbl_8 = 0.05 * jax.random.normal(jax.random.fold_in(_tk, 500 + 8), (1000, 16), jnp.float32)
        tbl_9 = 0.05 * jax.random.normal(jax.random.fold_in(_tk, 500 + 9), (12500, 16), jnp.float32)
        tbl_10 = 0.05 * jax.random.normal(jax.random.fold_in(_tk, 500 + 10), (125000, 16), jnp.float32)
        tbl_11 = 0.05 * jax.random.normal(jax.random.fold_in(_tk, 500 + 11), (12500, 16), jnp.float32)
        tbl_12 = 0.05 * jax.random.normal(jax.random.fold_in(_tk, 500 + 12), (1000, 16), jnp.float32)
        tbl_13 = 0.05 * jax.random.normal(jax.random.fold_in(_tk, 500 + 13), (1250, 16), jnp.float32)
        tbl_14 = 0.05 * jax.random.normal(jax.random.fold_in(_tk, 500 + 14), (1000, 16), jnp.float32)
        tbl_15 = 0.05 * jax.random.normal(jax.random.fold_in(_tk, 500 + 15), (125000, 16), jnp.float32)
        tbl_16 = 0.05 * jax.random.normal(jax.random.fold_in(_tk, 500 + 16), (1000, 16), jnp.float32)
        tbl_17 = 0.05 * jax.random.normal(jax.random.fold_in(_tk, 500 + 17), (1250, 16), jnp.float32)
        tbl_18 = 0.05 * jax.random.normal(jax.random.fold_in(_tk, 500 + 18), (12500, 16), jnp.float32)
        tbl_19 = 0.05 * jax.random.normal(jax.random.fold_in(_tk, 500 + 19), (1250, 16), jnp.float32)
        tbl_20 = 0.05 * jax.random.normal(jax.random.fold_in(_tk, 500 + 20), (1250, 16), jnp.float32)
        tbl_21 = 0.05 * jax.random.normal(jax.random.fold_in(_tk, 500 + 21), (125000, 16), jnp.float32)
        tbl_22 = 0.05 * jax.random.normal(jax.random.fold_in(_tk, 500 + 22), (12500, 16), jnp.float32)
        tbl_23 = 0.05 * jax.random.normal(jax.random.fold_in(_tk, 500 + 23), (1000, 16), jnp.float32)
        tbl_24 = 0.05 * jax.random.normal(jax.random.fold_in(_tk, 500 + 24), (125000, 16), jnp.float32)
        tbl_25 = 0.05 * jax.random.normal(jax.random.fold_in(_tk, 500 + 25), (125000, 16), jnp.float32)
        tbl_26 = 0.05 * jax.random.normal(jax.random.fold_in(_tk, 500 + 26), (12500, 16), jnp.float32)
        tbl_27 = 0.05 * jax.random.normal(jax.random.fold_in(_tk, 500 + 27), (1250, 16), jnp.float32)
        tbl_28 = 0.05 * jax.random.normal(jax.random.fold_in(_tk, 500 + 28), (1250, 16), jnp.float32)
        tbl_29 = 0.05 * jax.random.normal(jax.random.fold_in(_tk, 500 + 29), (1000, 16), jnp.float32)
        tbl_30 = 0.05 * jax.random.normal(jax.random.fold_in(_tk, 500 + 30), (125000, 16), jnp.float32)
        tbl_31 = 0.05 * jax.random.normal(jax.random.fold_in(_tk, 500 + 31), (1000, 16), jnp.float32)
        tbl_32 = 0.05 * jax.random.normal(jax.random.fold_in(_tk, 500 + 32), (1250, 16), jnp.float32)
        tbl_33 = 0.05 * jax.random.normal(jax.random.fold_in(_tk, 500 + 33), (125000, 16), jnp.float32)
        tbl_34 = 0.05 * jax.random.normal(jax.random.fold_in(_tk, 500 + 34), (1000, 16), jnp.float32)
        tbl_35 = 0.05 * jax.random.normal(jax.random.fold_in(_tk, 500 + 35), (1000, 16), jnp.float32)
        tbl_36 = 0.05 * jax.random.normal(jax.random.fold_in(_tk, 500 + 36), (1250, 16), jnp.float32)
        tbl_37 = 0.05 * jax.random.normal(jax.random.fold_in(_tk, 500 + 37), (125000, 16), jnp.float32)
        tbl_38 = 0.05 * jax.random.normal(jax.random.fold_in(_tk, 500 + 38), (1250, 16), jnp.float32)
        _rk = jax.random.fold_in(_tk, 7)
        W_top1 = 0.0606339 * jax.random.normal(jax.random.fold_in(_tk, 801), (272, 512), jnp.float32)
        W_top2 = 0.0441942 * jax.random.normal(jax.random.fold_in(_tk, 802), (512, 256), jnp.float32)
        W_top3 = 0.0625 * jax.random.normal(jax.random.fold_in(_tk, 803), (256, 1), jnp.float32)
        b_top1 = jnp.zeros((512,), jnp.float32)
        b_top2 = jnp.zeros((256,), jnp.float32)
        return (dense_ctx, ids, tbl_0, tbl_1, tbl_2, tbl_3, tbl_4, tbl_5, tbl_6, tbl_7, tbl_8, tbl_9, tbl_10, tbl_11, tbl_12, tbl_13, tbl_14, tbl_15, tbl_16, tbl_17, tbl_18, tbl_19, tbl_20, tbl_21, tbl_22, tbl_23, tbl_24, tbl_25, tbl_26, tbl_27, tbl_28, tbl_29, tbl_30, tbl_31, tbl_32, tbl_33, tbl_34, tbl_35, tbl_36, tbl_37, tbl_38, W_top1, b_top1, W_top2, b_top2, W_top3)
    dense_ctx, ids, tbl_0, tbl_1, tbl_2, tbl_3, tbl_4, tbl_5, tbl_6, tbl_7, tbl_8, tbl_9, tbl_10, tbl_11, tbl_12, tbl_13, tbl_14, tbl_15, tbl_16, tbl_17, tbl_18, tbl_19, tbl_20, tbl_21, tbl_22, tbl_23, tbl_24, tbl_25, tbl_26, tbl_27, tbl_28, tbl_29, tbl_30, tbl_31, tbl_32, tbl_33, tbl_34, tbl_35, tbl_36, tbl_37, tbl_38, W_top1, b_top1, W_top2, b_top2, W_top3 = _rec_inputs()

    def _L0_rec_setup():
        import jax, jax.numpy as jnp
        import numpy as np
        LAYER_SIZES = [128, 128, 128]
        F0 = 39
        D = 16
        B = 256
        key = jax.random.key(seed)
        ks = jax.random.split(key, 4)
        field_nums = [F0, LAYER_SIZES[0] // 2, LAYER_SIZES[1] // 2]
        x = jax.random.normal(ks[0], (B, F0, D), dtype=jnp.float32)
        W0 = jax.random.normal(ks[1], (F0 * field_nums[0], LAYER_SIZES[0]), dtype=jnp.float32) * 0.05
        W1 = jax.random.normal(ks[2], (F0 * field_nums[1], LAYER_SIZES[1]), dtype=jnp.float32) * 0.05
        W2 = jax.random.normal(ks[3], (F0 * field_nums[2], LAYER_SIZES[2]), dtype=jnp.float32) * 0.05
        b0 = jnp.zeros((LAYER_SIZES[0],), jnp.float32)
        b1 = jnp.zeros((LAYER_SIZES[1],), jnp.float32)
        b2 = jnp.zeros((LAYER_SIZES[2],), jnp.float32)
        return {'x': x, 'W0': W0, 'W1': W1, 'W2': W2, 'b0': b0, 'b1': b1, 'b2': b2}
    _L0_rec_all = _L0_rec_setup()
    _L0_rec_in = {k: v for k, v in _L0_rec_all.items() if k in ('W0', 'W1', 'W2', 'b0', 'b1', 'b2')}
    del _L0_rec_all
    return {'dense_ctx': dense_ctx, 'ids': ids, 'tbl_0': tbl_0, 'tbl_1': tbl_1, 'tbl_2': tbl_2, 'tbl_3': tbl_3, 'tbl_4': tbl_4, 'tbl_5': tbl_5, 'tbl_6': tbl_6, 'tbl_7': tbl_7, 'tbl_8': tbl_8, 'tbl_9': tbl_9, 'tbl_10': tbl_10, 'tbl_11': tbl_11, 'tbl_12': tbl_12, 'tbl_13': tbl_13, 'tbl_14': tbl_14, 'tbl_15': tbl_15, 'tbl_16': tbl_16, 'tbl_17': tbl_17, 'tbl_18': tbl_18, 'tbl_19': tbl_19, 'tbl_20': tbl_20, 'tbl_21': tbl_21, 'tbl_22': tbl_22, 'tbl_23': tbl_23, 'tbl_24': tbl_24, 'tbl_25': tbl_25, 'tbl_26': tbl_26, 'tbl_27': tbl_27, 'tbl_28': tbl_28, 'tbl_29': tbl_29, 'tbl_30': tbl_30, 'tbl_31': tbl_31, 'tbl_32': tbl_32, 'tbl_33': tbl_33, 'tbl_34': tbl_34, 'tbl_35': tbl_35, 'tbl_36': tbl_36, 'tbl_37': tbl_37, 'tbl_38': tbl_38, 'W_top1': W_top1, 'b_top1': b_top1, 'W_top2': W_top2, 'b_top2': b_top2, 'W_top3': W_top3, 'L0_rec_W0': _L0_rec_in['W0'], 'L0_rec_W1': _L0_rec_in['W1'], 'L0_rec_W2': _L0_rec_in['W2'], 'L0_rec_b0': _L0_rec_in['b0'], 'L0_rec_b1': _L0_rec_in['b1'], 'L0_rec_b2': _L0_rec_in['b2']}

def reference(dense_ctx, ids, tbl_0, tbl_1, tbl_2, tbl_3, tbl_4, tbl_5, tbl_6, tbl_7, tbl_8, tbl_9, tbl_10, tbl_11, tbl_12, tbl_13, tbl_14, tbl_15, tbl_16, tbl_17, tbl_18, tbl_19, tbl_20, tbl_21, tbl_22, tbl_23, tbl_24, tbl_25, tbl_26, tbl_27, tbl_28, tbl_29, tbl_30, tbl_31, tbl_32, tbl_33, tbl_34, tbl_35, tbl_36, tbl_37, tbl_38, W_top1, b_top1, W_top2, b_top2, W_top3, L0_rec_W0, L0_rec_W1, L0_rec_W2, L0_rec_b0, L0_rec_b1, L0_rec_b2):
    import jax
    import jax.numpy as jnp

    def _L0_rec_ref(x, W0, W1, W2, b0, b1, b2):
        import jax, jax.numpy as jnp
        import numpy as np
        LAYER_SIZES = [128, 128, 128]
        F0 = 39
        D = 16
        B = 256
        Ws = [W0, W1, W2]
        bs = [b0, b1, b2]
        h = x
        outs = []
        n_layers = len(LAYER_SIZES)
        for i, S in enumerate(LAYER_SIZES):
            Fk = h.shape[1]
            Wr = Ws[i].reshape(F0, Fk, S)
            out = jax.nn.relu(jnp.einsum('bfd,bgd,fgs->bsd', x, h, Wr) + bs[i][None, :, None])
            if i != n_layers - 1:
                h, direct = (out[:, :S // 2], out[:, S // 2:])
            else:
                direct = out
            outs.append(direct)
        result = jnp.concatenate(outs, axis=1)
        return jnp.sum(result, axis=-1)
    e = jnp.stack([tbl_0[ids[:, 0]], tbl_1[ids[:, 1]], tbl_2[ids[:, 2]], tbl_3[ids[:, 3]], tbl_4[ids[:, 4]], tbl_5[ids[:, 5]], tbl_6[ids[:, 6]], tbl_7[ids[:, 7]], tbl_8[ids[:, 8]], tbl_9[ids[:, 9]], tbl_10[ids[:, 10]], tbl_11[ids[:, 11]], tbl_12[ids[:, 12]], tbl_13[ids[:, 13]], tbl_14[ids[:, 14]], tbl_15[ids[:, 15]], tbl_16[ids[:, 16]], tbl_17[ids[:, 17]], tbl_18[ids[:, 18]], tbl_19[ids[:, 19]], tbl_20[ids[:, 20]], tbl_21[ids[:, 21]], tbl_22[ids[:, 22]], tbl_23[ids[:, 23]], tbl_24[ids[:, 24]], tbl_25[ids[:, 25]], tbl_26[ids[:, 26]], tbl_27[ids[:, 27]], tbl_28[ids[:, 28]], tbl_29[ids[:, 29]], tbl_30[ids[:, 30]], tbl_31[ids[:, 31]], tbl_32[ids[:, 32]], tbl_33[ids[:, 33]], tbl_34[ids[:, 34]], tbl_35[ids[:, 35]], tbl_36[ids[:, 36]], tbl_37[ids[:, 37]], tbl_38[ids[:, 38]]], axis=1)
    z = _L0_rec_ref(e, L0_rec_W0, L0_rec_W1, L0_rec_W2, L0_rec_b0, L0_rec_b1, L0_rec_b2)
    z = z.reshape(z.shape[0], -1)
    h = jnp.concatenate([z, dense_ctx], axis=1)
    h = jnp.maximum(h @ W_top1 + b_top1, 0.0)
    h = jnp.maximum(h @ W_top2 + b_top2, 0.0)
    y = h @ W_top3
    return y

_drawn_inputs = setup_inputs


def setup_inputs(seed=0):
    import zlib

    import numpy as np

    out = dict(_drawn_inputs(seed))
    spreads = {'b_top1': (0.0, 0.8),
     'b_top2': (0.0, 0.8),
     'L0_rec_b0': (0.0, 0.309),
     'L0_rec_b1': (0.0, 0.461),
     'L0_rec_b2': (0.0, 0.276)}
    factors = {'tbl_0': 8.0,
     'tbl_1': 8.0,
     'tbl_2': 8.0,
     'tbl_3': 8.0,
     'tbl_4': 8.0,
     'tbl_5': 8.0,
     'tbl_6': 8.0,
     'tbl_7': 8.0,
     'tbl_8': 8.0,
     'tbl_9': 8.0,
     'tbl_10': 8.0,
     'tbl_11': 8.0,
     'tbl_12': 8.0,
     'tbl_13': 8.0,
     'tbl_14': 8.0,
     'tbl_15': 8.0,
     'tbl_16': 8.0,
     'tbl_17': 8.0,
     'tbl_18': 8.0,
     'tbl_19': 8.0,
     'tbl_20': 8.0,
     'tbl_21': 8.0,
     'tbl_22': 7.229,
     'tbl_23': 8.0,
     'tbl_24': 8.0,
     'tbl_25': 8.0,
     'tbl_26': 8.0,
     'tbl_27': 8.0,
     'tbl_28': 8.0,
     'tbl_29': 8.0,
     'tbl_30': 8.0,
     'tbl_31': 7.126,
     'tbl_32': 8.0,
     'tbl_33': 8.0,
     'tbl_34': 8.0,
     'tbl_35': 8.0,
     'tbl_36': 8.0,
     'tbl_37': 8.0,
     'tbl_38': 8.0,
     'L0_rec_W0': 6.558,
     'L0_rec_W1': 3.266,
     'dense_ctx': 5.762}
    for name, (base, spread) in spreads.items():
        noise = np.random.default_rng([zlib.crc32(name.encode()), seed]).standard_normal(out[name].shape)
        drawn = base * np.exp(spread * noise) if base else spread * noise
        out[name] = jnp.asarray(drawn.astype(out[name].dtype))
    for name, factor in factors.items():
        out[name] = (out[name] * factor).astype(out[name].dtype)
    return out
```

```python
from contextlib import ExitStack

import numpy as np
import concourse.bass as bass
from concourse import mybir

F32 = mybir.dt.float32
I32 = mybir.dt.int32
ALU = mybir.AluOpType
ACT = mybir.ActivationFunctionType
AX = mybir.AxisListType

P = 128
BATCH = 2048
FIELDS = 39
DIM = 16
TILES = BATCH // P
DB = 4
BPT = DIM // DB
BLOCKS = TILES * BPT
COLS = DB * P
LAYER = 128
HIDDEN = LAYER // 2
DELTAS = 3
OFFSETS = FIELDS // 2 + 1
K0 = -(-OFFSETS // DELTAS)
ROWS0 = FIELDS * DELTAS
FQ = 4
GB = 32
KF = -(-FIELDS // FQ)
NG = HIDDEN // GB
XROWS = FIELDS + K0 * DELTAS - 1
PAIR = 2
S0 = -(-K0 // PAIR)
SG = KF // PAIR
SL = NG * SG
STEP_SLOTS = S0 + 2 * SL
RING = 8
SCR = 4
DENSE = 16
H1, H2 = 512, 256
M1, M2 = H1 // P, H2 // P
assert STEP_SLOTS % RING == 0 and KF % PAIR == 0 and BPT == 4 and SCR == BPT


def first_slot(layer, m):
    peeled = isinstance(m, int)
    base0 = 2 * S0 + SL
    last = base0 + STEP_SLOTS * (BLOCKS - 2)
    if layer == 0:
        if peeled and m < 2:
            return m * S0
        return m * STEP_SLOTS + (base0 - 2 * STEP_SLOTS)
    if layer == 1:
        if peeled and m == 0:
            return 2 * S0
        if peeled and m == BLOCKS - 1:
            return last
        return m * STEP_SLOTS + (base0 - STEP_SLOTS + S0)
    if peeled and m == BLOCKS - 2:
        return last + SL
    if peeled and m == BLOCKS - 1:
        return last + 2 * SL
    return m * STEP_SLOTS + (base0 + S0 + SL)


def group_index(layer, m):
    peeled = isinstance(m, int)
    if layer == 0:
        return m if peeled and m < 2 else m * 3 - 3
    if layer == 1:
        if peeled and m == 0:
            return 2
        return 3 * m if peeled and m == BLOCKS - 1 else m * 3 + 1
    if peeled and m >= BLOCKS - 2:
        return 3 * (BLOCKS - 1) + 1 + (m - (BLOCKS - 2))
    return m * 3 + 5


def shift_count(m, r):
    return (m - r % 2) * (8 * K0) + 16 * K0


def copy_count(m, r):
    return (m - r % SCR) * (16 * FQ // SCR) + 16 * FQ


def build(nc, ids, tables, dense_t, w0a, w0b, w1, w2, b_cin, wt1, bt1, wt2, bt2, wt3, y):
    with ExitStack() as ctx:
        def sb(name, shape, dt=F32):
            return ctx.enter_context(nc.sbuf_tensor(name, shape, dt))

        def ps(name, shape):
            return ctx.enter_context(nc.psum_tensor(name, shape, F32))

        def sem(name):
            return ctx.enter_context(nc.semaphore(name))

        x_scratch = nc.dram_tensor("x_scratch", (SCR, XROWS, COLS), F32)

        ids_all = sb("ids_all", [P, TILES * FIELDS], I32)
        ids_tile = sb("ids_tile", [P, FIELDS], I32)
        emb = sb("emb", [P, FIELDS * DIM])
        emb_rep = sb("emb_rep", [P, DIM, ROWS0])
        ident = sb("ident", [P, P])
        x_t = sb("x_t", [ROWS0, 2, COLS])
        x_shift = sb("x_shift", [ROWS0, 2, K0, COLS])
        x_copy = sb("x_copy", [P, SCR, KF, COLS])
        prod = sb("prod", [P, RING, PAIR, COLS])
        w0_sb = sb("w0_sb", [ROWS0, K0, LAYER])
        w1_sb = sb("w1_sb", [P, NG, KF, LAYER])
        w2_sb = sb("w2_sb", [P, NG, KF, LAYER])
        b_sb = sb("b_sb", [P, 3])
        direct01 = sb("direct01", [P, 2, COLS])
        direct2 = sb("direct2", [P, 2, COLS])
        part01 = sb("part01", [P, BPT, P])
        part2 = sb("part2", [P, BPT, P])
        z01 = sb("z01", [P, P])
        z2 = sb("z2", [P, P])
        dense_sb = sb("dense_sb", [DENSE, P])
        wt1_z = sb("wt1_z", [P, 2, H1])
        wt1_d = sb("wt1_d", [DENSE, H1])
        bt1_sb = sb("bt1_sb", [P, M1])
        wt2_sb = sb("wt2_sb", [P, M1, H2])
        bt2_sb = sb("bt2_sb", [P, M2])
        wt3_sb = sb("wt3_sb", [P, M2])
        h1 = sb("h1", [P, M1, P])
        h2 = sb("h2", [P, M2, P])
        y_sb = sb("y_sb", [1, P])

        x_rep = ps("x_rep", [ROWS0, COLS])
        hid = [ps(f"hid{layer}", [P, NG, COLS]) for layer in (1, 2)]
        acc = ps("acc", [P, 2, COLS])
        mlp = ps("mlp", [P, M1, P])

        ids_loaded = sem("ids_loaded")
        w_loaded = sem("w_loaded")
        mlp_w_loaded = sem("mlp_w_loaded")
        w0_summed = sem("w0_summed")
        ident_zeroed = sem("ident_zeroed")
        ident_ready = sem("ident_ready")
        ids_copied = sem("ids_copied")
        gathers_begun = sem("gathers_begun")
        gathered = sem("gathered")
        emb_copied = sem("emb_copied")
        transposed = sem("transposed")
        x_t_ready = sem("x_t_ready")
        scratch_written = sem("scratch_written")
        shift_loaded = [sem(f"shift_loaded{i}") for i in range(2)]
        copy_loaded = [sem(f"copy_loaded{i}") for i in range(SCR)]
        prod_ready = sem("prod_ready")
        prod_used = sem("prod_used")
        group_done = sem("group_done")
        group_read = sem("group_read")
        hidden_ready = [sem(f"hidden_ready{layer}") for layer in (1, 2)]
        reduced = sem("reduced")
        parts01 = sem("parts01")
        parts2 = sem("parts2")
        z01_ready = sem("z01_ready")
        z2_ready = sem("z2_ready")
        dense_loaded = sem("dense_loaded")
        mlp1_done = sem("mlp1_done")
        mlp2_done = sem("mlp2_done")
        mlp3_done = sem("mlp3_done")
        h1_ready = sem("h1_ready")
        h2_ready = sem("h2_ready")
        y_ready = sem("y_ready")
        y_written = sem("y_written")

        block = ctx.enter_context(nc.Block())

        def steps(eng, body):
            for r in range(BPT):
                body(r, r)
            with eng.Fori(1, TILES - 1) as t:
                for j in range(BPT):
                    body(t * BPT + j, 2 * BPT + j)
            for r in range(BLOCKS - BPT, BLOCKS):
                body(r, r)

        @block.sync
        def _(sp):
            sp.dma_start(ids_all[:, :], ids).then_inc(ids_loaded, 16)
            sp.dma_start(w0_sb[:, :, :], w0a).then_inc(w_loaded, 16)
            sp.dma_start(prod[0:ROWS0, 0:2, :, :].rearrange("p a b c -> p (a b c)")[:, 0:K0 * LAYER],
                         w0b).then_inc(w_loaded, 16)
            sp.dma_start(b_sb[:, :], b_cin).then_inc(w_loaded, 16)
            sp.dma_start(w1_sb[:, :, :, :], w1).then_inc(w_loaded, 16)
            sp.dma_start(w2_sb[:, :, :, :], w2).then_inc(w_loaded, 16)
            sp.dma_start(wt1_z[:, :, :], wt1[0:2 * P, :].rearrange("(k p) n -> p k n", p=P)).then_inc(mlp_w_loaded, 16)
            sp.dma_start(wt1_d[:, :], wt1[2 * P:2 * P + DENSE, :]).then_inc(mlp_w_loaded, 16)
            sp.dma_start(wt2_sb[:, :, :], wt2.rearrange("(k p) n -> p k n", p=P)).then_inc(mlp_w_loaded, 16)
            sp.dma_start(bt1_sb[:, :], bt1).then_inc(mlp_w_loaded, 16)
            sp.dma_start(bt2_sb[:, :], bt2).then_inc(mlp_w_loaded, 16)
            sp.dma_start(wt3_sb[:, :], wt3).then_inc(mlp_w_loaded, 16)

            def spread_block(m, r):
                slot = r % SCR
                sp.wait_ge(x_t_ready, m + 1)
                if r >= SCR:
                    sp.wait_ge(shift_loaded[r % 2], shift_count(m - SCR, r))
                    sp.wait_ge(copy_loaded[slot], copy_count(m - SCR, r))
                sp.dma_start(x_scratch.ap()[slot, 0:FIELDS, :],
                             x_t[0:ROWS0:DELTAS, r % 2, :]).then_inc(scratch_written, 16)
                sp.dma_start(x_scratch.ap()[slot, FIELDS:XROWS, :],
                             x_t[0:(XROWS - FIELDS) * DELTAS:DELTAS, r % 2, :]).then_inc(scratch_written, 16)
                sp.wait_ge(scratch_written, m * 32 + 32)
                if r >= 2:
                    sp.wait_ge(prod_ready, first_slot(0, m - 2) + S0)
                for k in range(K0):
                    src = bass.AP(tensor=x_scratch, offset=(slot * XROWS + k * DELTAS) * COLS,
                                  ap=[[COLS, FIELDS], [COLS, DELTAS], [1, COLS]])
                    sp.dma_start(x_shift[:, r % 2, k, :], src).then_inc(shift_loaded[r % 2], 16)
                if r >= SCR:
                    sp.wait_ge(prod_ready, first_slot(2, m - SCR) + SL)
                for q in range(FQ):
                    src = bass.AP(tensor=x_scratch, offset=(slot * XROWS + q) * COLS,
                                  ap=[[0, GB], [FQ * COLS, KF], [1, COLS]])
                    sp.dma_start(x_copy[q * GB:(q + 1) * GB, slot, :, :], src).then_inc(copy_loaded[slot], 16)

            def load_dense(t):
                first = t * P if isinstance(t, int) else sp.snap(t * P)
                if not (isinstance(t, int) and t == 0):
                    sp.wait_ge(mlp1_done, t)
                sp.dma_start(dense_sb[:, :], dense_t[:, bass.ds(first, P)]).then_inc(dense_loaded, 16)

            spread_block(0, 0)
            spread_block(1, 1)

            def step(n, r):
                if r < BLOCKS - 2:
                    spread_block(n + 2, r + 2)
                if r % BPT == 0 and r > 0:
                    load_dense(n // BPT - 1 if isinstance(n, int) else tile_of[0] - 1)

            tile_of = [None]
            for r in range(BPT):
                step(r, r)
            with sp.Fori(1, TILES - 1) as t:
                tile_of[0] = t
                for j in range(BPT):
                    step(t * BPT + j, 2 * BPT + j)
            for r in range(BLOCKS - BPT, BLOCKS):
                step(r, r)
            load_dense(TILES - 1)
            sp.wait_ge(scratch_written, 32 * BLOCKS)

        @block.gpsimd
        def _(pool):
            nc.gpsimd.memset(ident[:, :], 0.0).then_inc(ident_zeroed, 1)
            pool.wait_ge(ids_loaded, 16)

            def gather_tile(t, first):
                if not first:
                    pool.wait_ge(gathered, t * (16 * FIELDS))
                    pool.wait_ge(emb_copied, t)
                nc.gpsimd.tensor_copy(ids_tile[:, :], ids_all[:, bass.ds(t * FIELDS, FIELDS)]).then_inc(ids_copied, 1)
                pool.wait_ge(ids_copied, t + 1)
                pool.sem_inc(gathers_begun, 1)
                for f in range(FIELDS):
                    nc.gpsimd.indirect_dma_start(
                        out=emb[:, f * DIM:(f + 1) * DIM], out_offset=None, in_=tables[f],
                        in_offset=bass.IndirectOffsetOnAxis(ap=ids_tile[:, f:f + 1], axis=0),
                    ).then_inc(gathered, 16)

            gather_tile(0, True)
            pool.wait_ge(ident_zeroed, 1)
            nc.gpsimd.affine_select(out=ident[:, :], in_=ident[:, :], compare_op=ALU.not_equal, fill=1.0,
                                    base=0, pattern=[[-1, P]], channel_multiplier=1).then_inc(ident_ready, 1)
            with pool.Fori(1, TILES) as t:
                gather_tile(t, False)

        @block.scalar
        def _(act):
            def copy_emb(t):
                act.wait_ge(gathered, (t + 1) * (16 * FIELDS))
                if not (isinstance(t, int) and t == 0):
                    act.wait_ge(transposed, t * BPT)
                src = emb[:, :].rearrange("p (f d) -> p d f", d=DIM).unsqueeze(3).to_broadcast([P, DIM, FIELDS, DELTAS])
                dst = emb_rep[:, :, :].rearrange("p d (f j) -> p d f j", j=DELTAS)
                nc.scalar.activation(dst, src, ACT.Copy).then_inc(emb_copied, 1)

            def read_x(m, r):
                act.wait_ge(transposed, m + 1)
                if r >= 2:
                    act.wait_ge(scratch_written, (m - 1) * 32)
                nc.scalar.activation(x_t[:, r % 2, :], x_rep[:, :], ACT.Copy).then_inc(x_t_ready, 1)

            def read_group(layer, m, r):
                bank = acc[:, group_index(layer, r) % 2, :]
                act.wait_ge(group_done, group_index(layer, m) + 1)
                if layer < 2:
                    for g in range(NG):
                        if r >= 1:
                            act.wait_ge(prod_ready, first_slot(layer + 1, m - 1) + (g + 1) * SG)
                        for q in range(FQ):
                            last = nc.scalar.activation(
                                hid[layer][q * GB:(q + 1) * GB, g, :], bank[g * GB:(g + 1) * GB, :], ACT.Relu,
                                bias=b_sb[g * GB:(g + 1) * GB, layer:layer + 1])
                        last.then_inc(hidden_ready[layer], 1)
                    if layer == 0 and r >= 2:
                        act.wait_ge(reduced, m - 1)
                    nc.scalar.activation(direct01[layer * HIDDEN:(layer + 1) * HIDDEN, r % 2, :],
                                         bank[HIDDEN:LAYER, :], ACT.Relu,
                                         bias=b_sb[HIDDEN:LAYER, layer:layer + 1]).then_inc(group_read, 1)
                else:
                    if r >= 2:
                        act.wait_ge(parts2, m - 1)
                    nc.scalar.activation(direct2[:, r % 2, :], bank, ACT.Relu,
                                         bias=b_sb[:, layer:layer + 1]).then_inc(group_read, 1)

            def read_mlp1(t):
                act.wait_ge(mlp1_done, t + 1)
                for i in range(M1):
                    nc.scalar.activation(h1[:, i, :], mlp[:, i, :], ACT.Relu,
                                         bias=bt1_sb[:, i:i + 1]).then_inc(h1_ready, 1)

            def read_mlp2(t):
                act.wait_ge(mlp2_done, t + 1)
                for i in range(M2):
                    nc.scalar.activation(h2[:, i, :], mlp[:, i, :], ACT.Relu,
                                         bias=bt2_sb[:, i:i + 1]).then_inc(h2_ready, 1)

            def write_y(t):
                act.wait_ge(mlp3_done, t + 1)
                if not (isinstance(t, int) and t == 0):
                    act.wait_ge(y_written, t * 16)
                nc.scalar.activation(y_sb[:, :], mlp[0:1, M2, :], ACT.Copy).then_inc(y_ready, 1)
                act.wait_ge(y_ready, t + 1)
                act.dma_start(y[:, bass.ds(t * P, P)], y_sb[:, :]).then_inc(y_written, 16)

            copy_emb(0)
            read_x(0, 0)
            act.wait_ge(w_loaded, 16 * 5)
            read_group(0, 0, 0)
            read_x(1, 1)
            act.wait_ge(mlp_w_loaded, 16 * 6)

            def step(n, r, t):
                if r % BPT == 2 and r < BLOCKS - BPT:
                    copy_emb(t + 1)
                if r < BLOCKS - 1:
                    read_group(0, n + 1, r + 1)
                if r < BLOCKS - 2:
                    read_x(n + 2, r + 2)
                read_group(1, n, r)
                if r >= BPT and r % BPT == 2:
                    read_mlp1(t - 1)
                if r >= BPT and r % BPT == 3:
                    read_mlp2(t - 1)
                if r >= 1:
                    read_group(2, n - 1, r - 1)
                if r >= BPT and r % BPT == 3:
                    write_y(t - 1)

            for r in range(BPT):
                step(r, r, 0)
            with act.Fori(1, TILES - 1) as t:
                for j in range(BPT):
                    step(t * BPT + j, 2 * BPT + j, t)
            for r in range(BLOCKS - BPT, BLOCKS):
                step(r, r, TILES - 1)
            read_group(2, BLOCKS - 1, BLOCKS - 1)
            read_mlp1(TILES - 1)
            read_mlp2(TILES - 1)
            write_y(TILES - 1)
            act.wait_ge(y_written, 16 * TILES)

        @block.vector
        def _(dve):
            dve.wait_ge(w_loaded, 16 * 5)
            nc.vector.tensor_tensor(
                w0_sb[:, :, :], w0_sb[:, :, :],
                prod[0:ROWS0, 0:2, :, :].rearrange("p a b c -> p (a b c)")[:, 0:K0 * LAYER]
                .rearrange("p (k s) -> p k s", k=K0), ALU.add).then_inc(w0_summed, 1)
            dve.wait_ge(w0_summed, 1)

            def free_slot(layer, m, r, i):
                if first_slot(layer, r) + i >= RING:
                    dve.wait_ge(prod_used, first_slot(layer, m) + (i + 1 - RING))
                return (first_slot(layer, r) + i) % RING

            def products0(m, r):
                dve.wait_ge(shift_loaded[r % 2], shift_count(m, r))
                dve.wait_ge(transposed, m + 1)
                for i in range(S0):
                    k, n = i * PAIR, min(PAIR, K0 - i * PAIR)
                    slot = free_slot(0, m, r, i)
                    nc.vector.tensor_tensor(
                        prod[0:ROWS0, slot, 0:n, :],
                        x_rep[:, :].unsqueeze(1).to_broadcast([ROWS0, n, COLS]),
                        x_shift[:, r % 2, k:k + n, :], ALU.mult).then_inc(prod_ready, 1)

            def products(layer, m, r):
                dve.wait_ge(copy_loaded[r % SCR], copy_count(m, r))
                for g in range(NG):
                    dve.wait_ge(hidden_ready[layer - 1], m * NG + (g + 1))
                    for i in range(SG):
                        slot = free_slot(layer, m, r, g * SG + i)
                        nc.vector.tensor_tensor(
                            prod[:, slot, :, :],
                            hid[layer - 1][:, g, :].unsqueeze(1).to_broadcast([P, PAIR, COLS]),
                            x_copy[:, r % SCR, i * PAIR:(i + 1) * PAIR, :], ALU.mult).then_inc(prod_ready, 1)

            def sum_block(direct, half, part, slot):
                return nc.vector.tensor_reduce(
                    part[:, slot, :], direct[:, half, :].rearrange("p (d b) -> p b d", d=DB), AX.X, ALU.add)

            def sum_tile(part, z):
                return nc.vector.tensor_reduce(z[:, :], part[:, :, :].rearrange("p j b -> p b j"), AX.X, ALU.add)

            def sum01(m, r, t):
                dve.wait_ge(group_read, group_index(1, m) + 1)
                if r >= BPT and r % BPT == 0:
                    dve.wait_ge(z01_ready, t)
                sum_block(direct01, r % 2, part01, r % BPT).then_inc(reduced, 1)
                if r % BPT == BPT - 1:
                    dve.wait_ge(reduced, m + 1)
                    if r >= BPT:
                        dve.wait_ge(mlp1_done, t)
                    sum_tile(part01, z01).then_inc(z01_ready, 1)

            def sum2(m, r, t):
                dve.wait_ge(group_read, group_index(2, m) + 1)
                if r >= BPT and r % BPT == 0:
                    dve.wait_ge(z2_ready, t)
                sum_block(direct2, r % 2, part2, r % BPT).then_inc(parts2, 1)
                if r % BPT == BPT - 1:
                    dve.wait_ge(parts2, m + 1)
                    if r >= BPT:
                        dve.wait_ge(mlp1_done, t)
                    sum_tile(part2, z2).then_inc(z2_ready, 1)

            products0(0, 0)

            def step(n, r, t):
                if r < BLOCKS - 1:
                    products0(n + 1, r + 1)
                products(1, n, r)
                if r >= 1:
                    sum01(n - 1, r - 1, t if r % BPT >= 1 else t - 1)
                if r >= 2:
                    sum2(n - 2, r - 2, t if r % BPT >= 2 else t - 1)
                if r >= 1:
                    products(2, n - 1, r - 1)

            for r in range(BPT):
                step(r, r, 0)
            with dve.Fori(1, TILES - 1) as t:
                for j in range(BPT):
                    step(t * BPT + j, 2 * BPT + j, t)
            for r in range(BLOCKS - BPT, BLOCKS):
                step(r, r, TILES - 1)
            products(2, BLOCKS - 1, BLOCKS - 1)
            sum01(BLOCKS - 1, BLOCKS - 1, TILES - 1)
            sum2(BLOCKS - 2, BLOCKS - 2, TILES - 1)
            sum2(BLOCKS - 1, BLOCKS - 1, TILES - 1)

        @block.tensor
        def _(pe):
            def transpose_block(m, r, t):
                pe.wait_ge(emb_copied, t + 1)
                if r >= 1:
                    pe.wait_ge(prod_ready, first_slot(0, m - 1) + S0)
                    pe.wait_ge(x_t_ready, m)
                for d in range(DB):
                    last = nc.tensor.transpose(x_rep[:, d * P:(d + 1) * P], emb_rep[:, (r % BPT) * DB + d, :],
                                               ident[:, :])
                last.then_inc(transposed, 1)

            def contract(layer, m, r):
                bank = acc[:, group_index(layer, r) % 2, :]
                if group_index(layer, r) >= 2:
                    pe.wait_ge(group_read, group_index(layer, m) - 1)
                slots = S0 if layer == 0 else SL
                for i in range(slots):
                    slot = (first_slot(layer, r) + i) % RING
                    pe.wait_ge(prod_ready, first_slot(layer, m) + (i + 1))
                    n = min(PAIR, K0 - i * PAIR) if layer == 0 else PAIR
                    for e in range(n):
                        if layer == 0:
                            w, rhs = w0_sb[:, i * PAIR + e, :], prod[0:ROWS0, slot, e, :]
                        else:
                            w = (w1_sb, w2_sb)[layer - 1][:, i // SG, (i % SG) * PAIR + e, :]
                            rhs = prod[:, slot, e, :]
                        last = nc.tensor.matmul(bank, w, rhs, start=(i == 0 and e == 0),
                                                stop=(i == slots - 1 and e == n - 1))
                    last.then_inc(prod_used, 1)
                pe.wait_ge(prod_used, first_slot(layer, m) + slots)
                pe.sem_inc(group_done, 1)

            def mlp1(t, first):
                pe.wait_ge(z01_ready, t + 1)
                pe.wait_ge(z2_ready, t + 1)
                pe.wait_ge(dense_loaded, (t + 1) * 16)
                if not first:
                    pe.wait_ge(y_ready, t)
                for i in range(M1):
                    cols = slice(i * P, (i + 1) * P)
                    nc.tensor.matmul(mlp[:, i, :], wt1_z[:, 0, cols], z01[:, :], start=True, stop=False)
                    nc.tensor.matmul(mlp[:, i, :], wt1_z[:, 1, cols], z2[:, :], start=False, stop=False)
                    last = nc.tensor.matmul(mlp[:, i, :], wt1_d[:, cols], dense_sb[:, :], start=False, stop=True)
                last.then_inc(mlp1_done, 1)

            def mlp2(t):
                pe.wait_ge(h1_ready, (t + 1) * M1)
                for i in range(M2):
                    for k in range(M1):
                        last = nc.tensor.matmul(mlp[:, i, :], wt2_sb[:, k, i * P:(i + 1) * P], h1[:, k, :],
                                                start=(k == 0), stop=(k == M1 - 1))
                last.then_inc(mlp2_done, 1)

            def mlp3(t):
                pe.wait_ge(h2_ready, (t + 1) * M2)
                for k in range(M2):
                    last = nc.tensor.matmul(mlp[0:1, M2, :], wt3_sb[:, k:k + 1], h2[:, k, :],
                                            start=(k == 0), stop=(k == M2 - 1))
                last.then_inc(mlp3_done, 1)

            pe.wait_ge(ident_ready, 1)
            transpose_block(0, 0, 0)
            pe.wait_ge(w0_summed, 1)
            contract(0, 0, 0)
            transpose_block(1, 1, 0)
            pe.wait_ge(mlp_w_loaded, 16 * 6)

            def step(n, r, t):
                if r < BLOCKS - 1:
                    contract(0, n + 1, r + 1)
                if r < BLOCKS - 2:
                    transpose_block(n + 2, r + 2, t if r % BPT < 2 else t + 1)
                contract(1, n, r)
                if r >= BPT and r % BPT == 2:
                    mlp1(t - 1, r == BPT + 2)
                if r >= BPT and r % BPT == 3:
                    mlp2(t - 1)
                if r >= 1:
                    contract(2, n - 1, r - 1)
                if r >= BPT and r % BPT == 3:
                    mlp3(t - 1)

            for r in range(BPT):
                step(r, r, 0)
            with pe.Fori(1, TILES - 1) as t:
                for j in range(BPT):
                    step(t * BPT + j, 2 * BPT + j, t)
            for r in range(BLOCKS - BPT, BLOCKS):
                step(r, r, TILES - 1)
            contract(2, BLOCKS - 1, BLOCKS - 1)
            mlp1(TILES - 1, False)
            mlp2(TILES - 1)
            mlp3(TILES - 1)


def kernel(**inputs):
    import concourse.bacc as bacc
    from concourse.bass_utils import run_bass_kernel_spmd

    nc = bacc.Bacc("TRN2", target_bir_lowering=False, num_devices=1)
    arrays = {}

    def given(name, a):
        a = np.ascontiguousarray(a)
        arrays[name] = a
        return nc.dram_tensor(name, a.shape, mybir.dt.from_np(a.dtype), kind="ExternalInput").ap()

    def arr(name):
        return np.asarray(inputs[name])

    ids = given("ids_in", arr("ids").reshape(TILES, P, FIELDS).transpose(1, 0, 2).reshape(P, TILES * FIELDS))
    tables = [given(f"tbl_{f}_in", arr(f"tbl_{f}")) for f in range(FIELDS)]
    dense_t = given("dense_t_in", arr("dense_ctx").T)

    w = arr("L0_rec_W0").reshape(FIELDS, FIELDS, LAYER)
    pairs = [np.zeros((FIELDS, DELTAS, K0, LAYER), w.dtype) for _ in range(2)]
    fields = np.arange(FIELDS)
    for k in range(K0):
        for j in range(DELTAS):
            delta = k * DELTAS + j
            if delta < OFFSETS:
                pairs[0][:, j, k] = w[fields, (fields + delta) % FIELDS]
                if delta > 0:
                    pairs[1][:, j, k] = w[(fields + delta) % FIELDS, fields]
    w0a = given("w0a_in", pairs[0].reshape(ROWS0, K0, LAYER))
    w0b = given("w0b_in", pairs[1].reshape(ROWS0, K0 * LAYER))

    def by_tile(w):
        full = np.zeros((KF * FQ, HIDDEN, LAYER), w.dtype)
        full[:FIELDS] = w.reshape(FIELDS, HIDDEN, LAYER)
        return full.reshape(KF, FQ, NG, GB, LAYER).transpose(1, 3, 2, 0, 4).reshape(P, NG, KF, LAYER)

    w1 = given("w1_in", by_tile(arr("L0_rec_W1")))
    w2 = given("w2_in", by_tile(arr("L0_rec_W2")))
    b_cin = given("b_cin_in", np.stack([arr(f"L0_rec_b{i}") for i in range(3)], axis=1))
    wt1 = given("wt1_in", arr("W_top1"))
    bt1 = given("bt1_in", arr("b_top1").reshape(M1, P).T)
    wt2 = given("wt2_in", arr("W_top2"))
    bt2 = given("bt2_in", arr("b_top2").reshape(M2, P).T)
    wt3 = given("wt3_in", arr("W_top3").reshape(M2, P).T)
    y = nc.dram_tensor("y_out", (1, BATCH), F32, kind="ExternalOutput").ap()

    build(nc, ids, tables, dense_t, w0a, w0b, w1, w2, b_cin, wt1, bt1, wt2, bt2, wt3, y)
    result = run_bass_kernel_spmd(nc, [arrays], core_ids=[0])
    return result.results[0]["y_out"].reshape(BATCH, 1)
```

```python
from contextlib import ExitStack

import numpy as np
import concourse.bass as bass
from concourse import mybir

F32 = mybir.dt.float32
F32R = mybir.dt.float32r
I32 = mybir.dt.int32
ALU = mybir.AluOpType
ACT = mybir.ActivationFunctionType
AX = mybir.AxisListType

P = 128
BATCH = 2048
FIELDS = 39
DIM = 16
TILES = BATCH // P
DB = 4
BPT = DIM // DB
BLOCKS = TILES * BPT
COLS = DB * P
LAYER = 128
HIDDEN = LAYER // 2
DELTAS = 3
OFFSETS = FIELDS // 2 + 1
K0 = -(-OFFSETS // DELTAS)
ROWS0 = FIELDS * DELTAS
FQ = 4
GB = 32
KF = -(-FIELDS // FQ)
NG = HIDDEN // GB
XROWS = FIELDS + K0 * DELTAS - 1
PAIR = 2
S0 = -(-K0 // PAIR)
SG = KF // PAIR
SL = NG * SG
STEP_SLOTS = S0 + 2 * SL
RING = 8
SPLIT = tuple(i for i in range(SL) if i % 2)
WHOLE = tuple(i for i in range(SL) if i not in SPLIT)
SPLIT_RING = 5
ALL_SLOTS, WHOLE_SLOTS, SPLIT_SLOTS = (S0, SL), (S0, len(WHOLE)), (0, len(SPLIT))
GATHERS = (10, 10, 10, 9)
SCR = 4
XC = 2
DENSE = 16
H1, H2 = 512, 256
M1, M2 = H1 // P, H2 // P
assert STEP_SLOTS % RING == 0 and 2 * len(SPLIT) % SPLIT_RING == 0 and sum(GATHERS) == FIELDS and KF % PAIR == 0 and BPT == 4 and SCR == BPT


def first_slot(layer, m, slots=ALL_SLOTS):
    s0, sl = slots
    peeled = isinstance(m, int)
    step_slots = s0 + 2 * sl
    base0 = 2 * s0 + sl
    last = base0 + step_slots * (BLOCKS - 2)
    if layer == 0:
        if peeled and m < 2:
            return m * s0
        return m * step_slots + (base0 - 2 * step_slots)
    if layer == 1:
        if peeled and m == 0:
            return 2 * s0
        if peeled and m == BLOCKS - 1:
            return last
        return m * step_slots + (base0 - step_slots + s0)
    if peeled and m >= BLOCKS - 2:
        return last + (m - (BLOCKS - 3)) * sl
    return m * step_slots + (base0 + s0 + sl)


def group_index(layer, m):
    peeled = isinstance(m, int)
    if layer == 0:
        return m if peeled and m < 2 else m * 3 - 3
    if layer == 1:
        if peeled and m == 0:
            return 2
        return 3 * m if peeled and m == BLOCKS - 1 else m * 3 + 1
    if peeled and m >= BLOCKS - 2:
        return 3 * (BLOCKS - 1) + 1 + (m - (BLOCKS - 2))
    return m * 3 + 5


def build(nc, ids, tables, dense_t, w0a, w0b, w_whole, w_split, b_cin, wt1, bt1, wt2, bt2, wt3, y):
    with ExitStack() as ctx:
        def sb(name, shape, dt=F32):
            return ctx.enter_context(nc.sbuf_tensor(name, shape, dt))

        def ps(name, shape):
            return ctx.enter_context(nc.psum_tensor(name, shape, F32))

        def sem(name):
            return ctx.enter_context(nc.semaphore(name))

        x_scratch = nc.dram_tensor("x_scratch", (SCR, XROWS, COLS), F32)

        ids_all = sb("ids_all", [P, TILES * FIELDS], I32)
        ids_tile = sb("ids_tile", [P, FIELDS], I32)
        emb = sb("emb", [P, FIELDS * DIM])
        emb_rep = sb("emb_rep", [P, DIM, ROWS0])
        ident = sb("ident", [P, P])
        x_t = sb("x_t", [ROWS0, COLS])
        x_shift = sb("x_shift", [ROWS0, K0, COLS])
        x_copy = sb("x_copy", [P, XC, KF, COLS])
        prod = sb("prod", [P, RING, PAIR, COLS])
        prod_hi = sb("prod_hi", [P, SPLIT_RING, PAIR, COLS], F32R)
        prod_lo = sb("prod_lo", [P, SPLIT_RING, PAIR, COLS], F32R)
        w0_sb = sb("w0_sb", [ROWS0, K0, LAYER])
        w_sb = sb("w_sb", [P, 2, len(WHOLE), PAIR, LAYER])
        w_hi = sb("w_hi", [P, 2, len(SPLIT), PAIR, LAYER], F32R)
        w_lo = sb("w_lo", [P, 2, len(SPLIT), PAIR, LAYER], F32R)
        w_size = 2 * len(SPLIT) * PAIR * LAYER
        w_staged = x_copy[:, 1, :, :].rearrange("p k c -> p (k c)")[:, 0:w_size]
        b_sb = sb("b_sb", [P, 3])
        direct01 = sb("direct01", [P, 2, COLS])
        direct2 = sb("direct2", [P, COLS])
        part01 = sb("part01", [P, BPT, P])
        part2 = sb("part2", [P, BPT, P])
        z01 = sb("z01", [P, P])
        z2 = sb("z2", [P, P])
        dense_sb = sb("dense_sb", [DENSE, P])
        wt1_z = sb("wt1_z", [P, 2, H1])
        wt1_d = sb("wt1_d", [DENSE, H1])
        bt1_sb = sb("bt1_sb", [P, M1])
        wt2_sb = sb("wt2_sb", [P, M1, H2])
        bt2_sb = sb("bt2_sb", [P, M2])
        wt3_sb = sb("wt3_sb", [P, M2])
        h1 = sb("h1", [P, M1, P])
        h2 = sb("h2", [P, M2, P])
        y_sb = sb("y_sb", [1, P])

        x_rep = ps("x_rep", [ROWS0, COLS])
        hid = [ps(f"hid{layer}", [P, NG, COLS]) for layer in (1, 2)]
        acc = ps("acc", [P, 2, COLS])
        mlp = ps("mlp", [P, M1, P])

        ids_loaded = sem("ids_loaded")
        w_loaded = sem("w_loaded")
        mlp_w_loaded = sem("mlp_w_loaded")
        w0_summed = sem("w0_summed")
        w_rounded = sem("w_rounded")
        w_parted = sem("w_parted")
        ident_zeroed = sem("ident_zeroed")
        ident_ready = sem("ident_ready")
        ids_copied = sem("ids_copied")
        gathers_begun = sem("gathers_begun")
        gathered = sem("gathered")
        emb_copied = sem("emb_copied")
        transposed = sem("transposed")
        x_t_ready = sem("x_t_ready")
        scratch_written = sem("scratch_written")
        shift_loaded = sem("shift_loaded")
        copy_loaded = [sem(f"copy_loaded{i}") for i in range(SG)]
        prod_ready = sem("prod_ready")
        whole_used = sem("whole_used")
        hi_ready = sem("hi_ready")
        lo_ready = sem("lo_ready")
        split_used = sem("split_used")
        group_done = sem("group_done")
        group_read = sem("group_read")
        hidden_ready = [sem(f"hidden_ready{layer}") for layer in (1, 2)]
        reduced = sem("reduced")
        parts01 = sem("parts01")
        parts2 = sem("parts2")
        z01_ready = sem("z01_ready")
        z2_ready = sem("z2_ready")
        dense_loaded = sem("dense_loaded")
        mlp1_done = sem("mlp1_done")
        mlp2_done = sem("mlp2_done")
        mlp3_done = sem("mlp3_done")
        h1_ready = sem("h1_ready")
        h2_ready = sem("h2_ready")
        y_ready = sem("y_ready")
        y_written = sem("y_written")

        block = ctx.enter_context(nc.Block())

        def steps(eng, body):
            for r in range(BPT):
                body(r, r)
            with eng.Fori(1, TILES - 1) as t:
                for j in range(BPT):
                    body(t * BPT + j, 2 * BPT + j)
            for r in range(BLOCKS - BPT, BLOCKS):
                body(r, r)

        @block.sync
        def _(sp):
            sp.dma_start(ids_all[:, :], ids).then_inc(ids_loaded, 16)
            sp.dma_start(w0_sb[:, :, :], w0a).then_inc(w_loaded, 16)
            sp.dma_start(prod[0:ROWS0, 0:2, :, :].rearrange("p a b c -> p (a b c)")[:, 0:K0 * LAYER],
                         w0b).then_inc(w_loaded, 16)
            sp.dma_start(b_sb[:, :], b_cin).then_inc(w_loaded, 16)
            sp.dma_start(w_staged, w_split).then_inc(w_loaded, 16)
            sp.dma_start(w_sb[:, :, :, :, :].rearrange("p a b c d -> p (a b c d)"), w_whole).then_inc(w_loaded, 16)
            sp.dma_start(wt1_z[:, :, :], wt1[0:2 * P, :].rearrange("(k p) n -> p k n", p=P)).then_inc(mlp_w_loaded, 16)
            sp.dma_start(wt1_d[:, :], wt1[2 * P:2 * P + DENSE, :]).then_inc(mlp_w_loaded, 16)
            sp.dma_start(wt2_sb[:, :, :], wt2.rearrange("(k p) n -> p k n", p=P)).then_inc(mlp_w_loaded, 16)
            sp.dma_start(bt1_sb[:, :], bt1).then_inc(mlp_w_loaded, 16)
            sp.dma_start(bt2_sb[:, :], bt2).then_inc(mlp_w_loaded, 16)
            sp.dma_start(wt3_sb[:, :], wt3).then_inc(mlp_w_loaded, 16)

            def load_shift(m, r):
                slot = r % SCR
                sp.wait_ge(x_t_ready, m + 1)
                sp.dma_start(x_scratch.ap()[slot, 0:FIELDS, :],
                             x_t[0:ROWS0:DELTAS, :]).then_inc(scratch_written, 16)
                sp.dma_start(x_scratch.ap()[slot, FIELDS:XROWS, :],
                             x_t[0:(XROWS - FIELDS) * DELTAS:DELTAS, :]).then_inc(scratch_written, 16)
                sp.wait_ge(scratch_written, m * 32 + 32)
                if r >= 1:
                    sp.wait_ge(prod_ready, first_slot(0, m - 1) + S0)
                for k in range(K0):
                    src = bass.AP(tensor=x_scratch, offset=(slot * XROWS + k * DELTAS) * COLS,
                                  ap=[[COLS, FIELDS], [COLS, DELTAS], [1, COLS]])
                    sp.dma_start(x_shift[:, k, :], src).then_inc(shift_loaded, 16)

            def load_copies(m, r):
                if r == 1:
                    sp.wait_ge(w_parted, 1)
                for i in range(SG):
                    if r >= XC:
                        sp.wait_ge(prod_ready, first_slot(2, m - XC) + (SL - SG + i + 1))
                    for q in range(FQ):
                        src = bass.AP(tensor=x_scratch, offset=((r % SCR) * XROWS + i * PAIR * FQ + q) * COLS,
                                      ap=[[0, GB], [FQ * COLS, PAIR], [1, COLS]])
                        sp.dma_start(x_copy[q * GB:(q + 1) * GB, r % XC, i * PAIR:(i + 1) * PAIR, :],
                                     src).then_inc(copy_loaded[i], 16)

            def load_dense(t):
                first = t * P if isinstance(t, int) else sp.snap(t * P)
                if not (isinstance(t, int) and t == 0):
                    sp.wait_ge(mlp1_done, t)
                sp.dma_start(dense_sb[:, :], dense_t[:, bass.ds(first, P)]).then_inc(dense_loaded, 16)

            load_shift(0, 0)
            load_copies(0, 0)
            load_shift(1, 1)

            def step(n, r):
                if r < BLOCKS - 2:
                    load_shift(n + 2, r + 2)
                if r < BLOCKS - 1:
                    load_copies(n + 1, r + 1)
                if r % BPT == 0 and r > 0:
                    load_dense(n // BPT - 1 if isinstance(n, int) else tile_of[0] - 1)

            tile_of = [None]
            for r in range(BPT):
                step(r, r)
            with sp.Fori(1, TILES - 1) as t:
                tile_of[0] = t
                for j in range(BPT):
                    step(t * BPT + j, 2 * BPT + j)
            for r in range(BLOCKS - BPT, BLOCKS):
                step(r, r)
            load_dense(TILES - 1)
            sp.wait_ge(scratch_written, 32 * BLOCKS)

        @block.gpsimd
        def _(pool):
            nc.gpsimd.memset(ident[:, :], 0.0).then_inc(ident_zeroed, 1)
            pool.wait_ge(ids_loaded, 16)

            def take_ids(t):
                if not (isinstance(t, int) and t == 0):
                    pool.wait_ge(gathered, t * (16 * FIELDS))
                    pool.wait_ge(emb_copied, t)
                nc.gpsimd.tensor_copy(ids_tile[:, :], ids_all[:, bass.ds(t * FIELDS, FIELDS)]).then_inc(ids_copied, 1)
                pool.wait_ge(ids_copied, t + 1)
                pool.sem_inc(gathers_begun, 1)

            def gather(f):
                nc.gpsimd.indirect_dma_start(
                    out=emb[:, f * DIM:(f + 1) * DIM], out_offset=None, in_=tables[f],
                    in_offset=bass.IndirectOffsetOnAxis(ap=ids_tile[:, f:f + 1], axis=0),
                ).then_inc(gathered, 16)

            def part_slot(layer, m, r, e):
                pos = (first_slot(layer, r) + SPLIT[e]) % RING
                at = (first_slot(layer, r, SPLIT_SLOTS) + e) % SPLIT_RING
                pool.wait_ge(hi_ready, first_slot(layer, m, SPLIT_SLOTS) + (e + 1))
                nc.gpsimd.tensor_tensor(prod_lo[:, at, :, :], prod[:, pos, :, :],
                                        prod_hi[:, at, :, :].bitcast(F32), ALU.subtract).then_inc(lo_ready, 1)

            def step(n, r, t):
                if r < 2:
                    todo = [f for f in range(FIELDS) if f % 2 == r]
                elif r < BLOCKS - BPT - 2:
                    f = sum(GATHERS[:(r - 2) % BPT])
                    todo = list(range(f, f + GATHERS[(r - 2) % BPT]))
                else:
                    todo = []
                work = [(1, n, r, e) for e in range(len(SPLIT))]
                if r >= 1:
                    work += [(2, n - 1, r - 1, e) for e in range(len(SPLIT))]
                for i, w in enumerate(work):
                    part_slot(*w)
                    if i == 1 and todo and r % BPT == 2:
                        take_ids(t + 2)
                    if i >= 2 and todo:
                        gather(todo.pop(0))
                for f in todo:
                    gather(f)

            take_ids(0)
            for f in range(FIELDS):
                gather(f)
            pool.wait_ge(ident_zeroed, 1)
            nc.gpsimd.affine_select(out=ident[:, :], in_=ident[:, :], compare_op=ALU.not_equal, fill=1.0,
                                    base=0, pattern=[[-1, P]], channel_multiplier=1).then_inc(ident_ready, 1)
            take_ids(1)
            for r in range(BPT):
                step(r, r, 0)
            with pool.Fori(1, TILES - 2) as t:
                for j in range(BPT):
                    step(t * BPT + j, 2 * BPT + j, t)
            for r in range(BLOCKS - 2 * BPT, BLOCKS):
                step(r, r, r // BPT)
            for e in range(len(SPLIT)):
                part_slot(2, BLOCKS - 1, BLOCKS - 1, e)

        @block.scalar
        def _(act):
            def copy_emb(t):
                act.wait_ge(gathered, (t + 1) * (16 * FIELDS))
                if not (isinstance(t, int) and t == 0):
                    act.wait_ge(transposed, t * BPT)
                src = emb[:, :].rearrange("p (f d) -> p d f", d=DIM).unsqueeze(3).to_broadcast([P, DIM, FIELDS, DELTAS])
                dst = emb_rep[:, :, :].rearrange("p d (f j) -> p d f j", j=DELTAS)
                nc.scalar.activation(dst, src, ACT.Copy).then_inc(emb_copied, 1)

            def read_x(m, r):
                act.wait_ge(transposed, m + 1)
                if r >= 1:
                    act.wait_ge(scratch_written, m * 32)
                nc.scalar.activation(x_t[:, :], x_rep[:, :], ACT.Copy).then_inc(x_t_ready, 1)

            def read_hidden(layer, m, r, g):
                act.wait_ge(group_done, group_index(layer, m) + 1)
                if r >= 1:
                    act.wait_ge(prod_ready, first_slot(layer + 1, m - 1) + (g + 1) * SG)
                for q in range(FQ):
                    last = nc.scalar.activation(
                        hid[layer][q * GB:(q + 1) * GB, g, :],
                        acc[g * GB:(g + 1) * GB, group_index(layer, r) % 2, :], ACT.Relu,
                        bias=b_sb[g * GB:(g + 1) * GB, layer:layer + 1])
                last.then_inc(hidden_ready[layer], 1)

            def read_direct(layer, m, r):
                act.wait_ge(group_done, group_index(layer, m) + 1)
                bank = acc[:, group_index(layer, r) % 2, :]
                if layer < 2:
                    if layer == 0 and r >= 2:
                        act.wait_ge(reduced, m - 1)
                    nc.scalar.activation(direct01[layer * HIDDEN:(layer + 1) * HIDDEN, r % 2, :],
                                         bank[HIDDEN:LAYER, :], ACT.Relu,
                                         bias=b_sb[HIDDEN:LAYER, layer:layer + 1]).then_inc(group_read, 1)
                else:
                    if r >= 1:
                        act.wait_ge(parts2, m)
                    nc.scalar.activation(direct2[:, :], bank, ACT.Relu,
                                         bias=b_sb[:, layer:layer + 1]).then_inc(group_read, 1)

            def round_slots(layer, m, r, g):
                for e, i in enumerate(SPLIT):
                    if i // SG != g:
                        continue
                    pos = (first_slot(layer, r) + i) % RING
                    index = first_slot(layer, r, SPLIT_SLOTS) + e
                    act.wait_ge(prod_ready, first_slot(layer, m) + (i + 1))
                    if index >= SPLIT_RING:
                        act.wait_ge(split_used, first_slot(layer, m, SPLIT_SLOTS) + (e + 1 - SPLIT_RING))
                    nc.scalar.activation(prod_hi[:, index % SPLIT_RING, :, :], prod[:, pos, :, :],
                                         ACT.Copy).then_inc(hi_ready, 1)

            def read_mlp1(t):
                act.wait_ge(mlp1_done, t + 1)
                for i in range(M1):
                    nc.scalar.activation(h1[:, i, :], mlp[:, i, :], ACT.Relu,
                                         bias=bt1_sb[:, i:i + 1]).then_inc(h1_ready, 1)

            def read_mlp2(t):
                act.wait_ge(mlp2_done, t + 1)
                for i in range(M2):
                    nc.scalar.activation(h2[:, i, :], mlp[:, i, :], ACT.Relu,
                                         bias=bt2_sb[:, i:i + 1]).then_inc(h2_ready, 1)

            def write_y(t):
                act.wait_ge(mlp3_done, t + 1)
                if not (isinstance(t, int) and t == 0):
                    act.wait_ge(y_written, t * 16)
                nc.scalar.activation(y_sb[:, :], mlp[0:1, M2, :], ACT.Copy).then_inc(y_ready, 1)
                act.wait_ge(y_ready, t + 1)
                act.dma_start(y[:, bass.ds(t * P, P)], y_sb[:, :]).then_inc(y_written, 16)

            act.wait_ge(w_loaded, 16 * 5)
            nc.scalar.activation(w_hi[:, :, :, :, :].rearrange("p a b c d -> p (a b c d)"), w_staged,
                                 ACT.Copy).then_inc(w_rounded, 1)
            copy_emb(0)
            read_x(0, 0)
            read_hidden(0, 0, 0, 0)
            read_hidden(0, 0, 0, 1)
            read_direct(0, 0, 0)
            read_x(1, 1)
            act.wait_ge(mlp_w_loaded, 16 * 6)

            def step(n, r, t):
                if r >= 2:
                    read_direct(2, n - 2, r - 2)
                if r % BPT == 2 and r < BLOCKS - BPT:
                    copy_emb(t + 1)
                for g in range(NG):
                    round_slots(1, n, r, g)
                    if r < BLOCKS - 1:
                        read_hidden(0, n + 1, r + 1, g)
                if r < BLOCKS - 1:
                    read_direct(0, n + 1, r + 1)
                if r < BLOCKS - 2:
                    read_x(n + 2, r + 2)
                for g in range(NG):
                    if r >= 1:
                        round_slots(2, n - 1, r - 1, g)
                    read_hidden(1, n, r, g)
                read_direct(1, n, r)
                if r >= BPT and r % BPT == 2:
                    read_mlp1(t - 1)
                if r >= BPT and r % BPT == 3:
                    read_mlp2(t - 1)
                if r >= BPT and r % BPT == 3:
                    write_y(t - 1)

            for r in range(BPT):
                step(r, r, 0)
            with act.Fori(1, TILES - 1) as t:
                for j in range(BPT):
                    step(t * BPT + j, 2 * BPT + j, t)
            for r in range(BLOCKS - BPT, BLOCKS):
                step(r, r, TILES - 1)
            read_direct(2, BLOCKS - 2, BLOCKS - 2)
            for g in range(NG):
                round_slots(2, BLOCKS - 1, BLOCKS - 1, g)
            read_direct(2, BLOCKS - 1, BLOCKS - 1)
            read_mlp1(TILES - 1)
            read_mlp2(TILES - 1)
            write_y(TILES - 1)
            act.wait_ge(y_written, 16 * TILES)

        @block.vector
        def _(dve):
            dve.wait_ge(w_loaded, 16 * 5)
            nc.vector.tensor_tensor(
                w0_sb[:, :, :], w0_sb[:, :, :],
                prod[0:ROWS0, 0:2, :, :].rearrange("p a b c -> p (a b c)")[:, 0:K0 * LAYER]
                .rearrange("p (k s) -> p k s", k=K0), ALU.add).then_inc(w0_summed, 1)
            dve.wait_ge(w_rounded, 1)
            nc.vector.tensor_tensor(
                w_lo[:, :, :, :, :].rearrange("p a b c d -> p (a b c d)"), w_staged,
                w_hi[:, :, :, :, :].rearrange("p a b c d -> p (a b c d)").bitcast(F32),
                ALU.subtract).then_inc(w_parted, 1)
            dve.wait_ge(w0_summed, 1)

            def free_slot(layer, m, r, i):
                pos = first_slot(layer, r) + i
                if pos >= RING:
                    for layer2, back in [(a, b) for a in range(3) for b in range(-3, 3)]:
                        r2 = r + back
                        size = S0 if layer2 == 0 else SL
                        if 0 <= r2 < BLOCKS and 0 <= pos - RING - first_slot(layer2, r2) < size:
                            i2, m2 = pos - RING - first_slot(layer2, r2), m + back
                            break
                    if layer2 and i2 in SPLIT:
                        dve.wait_ge(lo_ready, first_slot(layer2, m2, SPLIT_SLOTS) + (SPLIT.index(i2) + 1))
                    else:
                        n = WHOLE.index(i2) if layer2 else i2
                        dve.wait_ge(whole_used, first_slot(layer2, m2, WHOLE_SLOTS) + (n + 1))
                return pos % RING

            def products0(m, r):
                dve.wait_ge(shift_loaded, (m + 1) * (16 * K0))
                dve.wait_ge(transposed, m + 1)
                for i in range(S0):
                    k, n = i * PAIR, min(PAIR, K0 - i * PAIR)
                    slot = free_slot(0, m, r, i)
                    nc.vector.tensor_tensor(
                        prod[0:ROWS0, slot, 0:n, :],
                        x_rep[:, :].unsqueeze(1).to_broadcast([ROWS0, n, COLS]),
                        x_shift[:, k:k + n, :], ALU.mult).then_inc(prod_ready, 1)

            def products(layer, m, r):
                for g in range(NG):
                    dve.wait_ge(hidden_ready[layer - 1], m * NG + (g + 1))
                    for i in range(SG):
                        if g == 0:
                            dve.wait_ge(copy_loaded[i], (m + 1) * (16 * FQ))
                        slot = free_slot(layer, m, r, g * SG + i)
                        nc.vector.tensor_tensor(
                            prod[:, slot, :, :],
                            hid[layer - 1][:, g, :].unsqueeze(1).to_broadcast([P, PAIR, COLS]),
                            x_copy[:, r % XC, i * PAIR:(i + 1) * PAIR, :], ALU.mult).then_inc(prod_ready, 1)

            def sum_block(direct, part, slot):
                return nc.vector.tensor_reduce(
                    part[:, slot, :], direct.rearrange("p (d b) -> p b d", d=DB), AX.X, ALU.add)

            def sum_tile(part, z):
                return nc.vector.tensor_reduce(z[:, :], part[:, :, :].rearrange("p j b -> p b j"), AX.X, ALU.add)

            def sum01(m, r, t):
                dve.wait_ge(group_read, group_index(1, m) + 1)
                if r >= BPT and r % BPT == 0:
                    dve.wait_ge(z01_ready, t)
                sum_block(direct01[:, r % 2, :], part01, r % BPT).then_inc(reduced, 1)
                if r % BPT == BPT - 1:
                    dve.wait_ge(reduced, m + 1)
                    if r >= BPT:
                        dve.wait_ge(mlp1_done, t)
                    sum_tile(part01, z01).then_inc(z01_ready, 1)

            def sum2(m, r, t):
                dve.wait_ge(group_read, group_index(2, m) + 1)
                if r >= BPT and r % BPT == 0:
                    dve.wait_ge(z2_ready, t)
                sum_block(direct2[:, :], part2, r % BPT).then_inc(parts2, 1)
                if r % BPT == BPT - 1:
                    dve.wait_ge(parts2, m + 1)
                    if r >= BPT:
                        dve.wait_ge(mlp1_done, t)
                    sum_tile(part2, z2).then_inc(z2_ready, 1)

            products0(0, 0)

            def step(n, r, t):
                if r < BLOCKS - 1:
                    products0(n + 1, r + 1)
                products(1, n, r)
                if r >= 1:
                    sum01(n - 1, r - 1, t if r % BPT >= 1 else t - 1)
                if r >= 2:
                    sum2(n - 2, r - 2, t if r % BPT >= 2 else t - 1)
                if r >= 1:
                    products(2, n - 1, r - 1)

            for r in range(BPT):
                step(r, r, 0)
            with dve.Fori(1, TILES - 1) as t:
                for j in range(BPT):
                    step(t * BPT + j, 2 * BPT + j, t)
            for r in range(BLOCKS - BPT, BLOCKS):
                step(r, r, TILES - 1)
            products(2, BLOCKS - 1, BLOCKS - 1)
            sum2(BLOCKS - 2, BLOCKS - 2, TILES - 1)
            sum01(BLOCKS - 1, BLOCKS - 1, TILES - 1)
            sum2(BLOCKS - 1, BLOCKS - 1, TILES - 1)

        @block.tensor
        def _(pe):
            def transpose_block(m, r, t):
                pe.wait_ge(emb_copied, t + 1)
                if r >= 1:
                    pe.wait_ge(prod_ready, first_slot(0, m - 1) + S0)
                    pe.wait_ge(x_t_ready, m)
                for d in range(DB):
                    last = nc.tensor.transpose(x_rep[:, d * P:(d + 1) * P], emb_rep[:, (r % BPT) * DB + d, :],
                                               ident[:, :])
                last.then_inc(transposed, 1)

            def contract(layer, m, r):
                bank = acc[:, group_index(layer, r) % 2, :]
                if group_index(layer, r) >= 2:
                    pe.wait_ge(group_read, group_index(layer, m) - 1)
                slots = S0 if layer == 0 else SL
                for i in range(slots):
                    slot = (first_slot(layer, r) + i) % RING
                    if layer and i in SPLIT:
                        e = SPLIT.index(i)
                        at = (first_slot(layer, r, SPLIT_SLOTS) + e) % SPLIT_RING
                        count = first_slot(layer, m, SPLIT_SLOTS) + (e + 1)
                        pe.wait_ge(hi_ready, count)
                        for k in range(PAIR):
                            for w in (w_hi, w_lo):
                                nc.tensor.matmul(bank, w[:, layer - 1, e, k, :], prod_hi[:, at, k, :],
                                                 start=False, stop=False)
                        pe.wait_ge(lo_ready, count)
                        for k in range(PAIR):
                            last = nc.tensor.matmul(bank, w_hi[:, layer - 1, e, k, :], prod_lo[:, at, k, :],
                                                    start=False, stop=(i == slots - 1 and k == PAIR - 1))
                        last.then_inc(split_used, 1)
                        continue
                    pe.wait_ge(prod_ready, first_slot(layer, m) + (i + 1))
                    n = min(PAIR, K0 - i * PAIR) if layer == 0 else PAIR
                    for k in range(n):
                        if layer == 0:
                            w, rhs = w0_sb[:, i * PAIR + k, :], prod[0:ROWS0, slot, k, :]
                        else:
                            w, rhs = w_sb[:, layer - 1, WHOLE.index(i), k, :], prod[:, slot, k, :]
                        last = nc.tensor.matmul(bank, w, rhs, start=(i == 0 and k == 0),
                                                stop=(i == slots - 1 and k == n - 1))
                    last.then_inc(whole_used, 1)
                if layer and slots - 1 in SPLIT:
                    pe.wait_ge(split_used, first_slot(layer, m, SPLIT_SLOTS) + len(SPLIT))
                else:
                    pe.wait_ge(whole_used, first_slot(layer, m, WHOLE_SLOTS) + (len(WHOLE) if layer else S0))
                pe.sem_inc(group_done, 1)

            def mlp1(t, first):
                pe.wait_ge(z01_ready, t + 1)
                pe.wait_ge(z2_ready, t + 1)
                pe.wait_ge(dense_loaded, (t + 1) * 16)
                if not first:
                    pe.wait_ge(y_ready, t)
                for i in range(M1):
                    cols = slice(i * P, (i + 1) * P)
                    nc.tensor.matmul(mlp[:, i, :], wt1_z[:, 0, cols], z01[:, :], start=True, stop=False)
                    nc.tensor.matmul(mlp[:, i, :], wt1_z[:, 1, cols], z2[:, :], start=False, stop=False)
                    last = nc.tensor.matmul(mlp[:, i, :], wt1_d[:, cols], dense_sb[:, :], start=False, stop=True)
                last.then_inc(mlp1_done, 1)

            def mlp2(t):
                pe.wait_ge(h1_ready, (t + 1) * M1)
                for i in range(M2):
                    for k in range(M1):
                        last = nc.tensor.matmul(mlp[:, i, :], wt2_sb[:, k, i * P:(i + 1) * P], h1[:, k, :],
                                                start=(k == 0), stop=(k == M1 - 1))
                last.then_inc(mlp2_done, 1)

            def mlp3(t):
                pe.wait_ge(h2_ready, (t + 1) * M2)
                for k in range(M2):
                    last = nc.tensor.matmul(mlp[0:1, M2, :], wt3_sb[:, k:k + 1], h2[:, k, :],
                                            start=(k == 0), stop=(k == M2 - 1))
                last.then_inc(mlp3_done, 1)

            pe.wait_ge(ident_ready, 1)
            transpose_block(0, 0, 0)
            pe.wait_ge(w0_summed, 1)
            contract(0, 0, 0)
            transpose_block(1, 1, 0)
            pe.wait_ge(mlp_w_loaded, 16 * 6)
            pe.wait_ge(w_parted, 1)

            def step(n, r, t):
                if r < BLOCKS - 1:
                    contract(0, n + 1, r + 1)
                if r < BLOCKS - 2:
                    transpose_block(n + 2, r + 2, t if r % BPT < 2 else t + 1)
                contract(1, n, r)
                if r >= BPT and r % BPT == 2:
                    mlp1(t - 1, r == BPT + 2)
                if r >= BPT and r % BPT == 3:
                    mlp2(t - 1)
                if r >= 1:
                    contract(2, n - 1, r - 1)
                if r >= BPT and r % BPT == 3:
                    mlp3(t - 1)

            for r in range(BPT):
                step(r, r, 0)
            with pe.Fori(1, TILES - 1) as t:
                for j in range(BPT):
                    step(t * BPT + j, 2 * BPT + j, t)
            for r in range(BLOCKS - BPT, BLOCKS):
                step(r, r, TILES - 1)
            contract(2, BLOCKS - 1, BLOCKS - 1)
            mlp1(TILES - 1, False)
            mlp2(TILES - 1)
            mlp3(TILES - 1)


def kernel(**inputs):
    import concourse.bacc as bacc
    from concourse.bass_utils import run_bass_kernel_spmd

    nc = bacc.Bacc("TRN2", target_bir_lowering=False, num_devices=1)
    arrays = {}

    def given(name, a):
        a = np.ascontiguousarray(a)
        arrays[name] = a
        return nc.dram_tensor(name, a.shape, mybir.dt.from_np(a.dtype), kind="ExternalInput").ap()

    def arr(name):
        return np.asarray(inputs[name])

    ids = given("ids_in", arr("ids").reshape(TILES, P, FIELDS).transpose(1, 0, 2).reshape(P, TILES * FIELDS))
    tables = [given(f"tbl_{f}_in", arr(f"tbl_{f}")) for f in range(FIELDS)]
    dense_t = given("dense_t_in", arr("dense_ctx").T)

    w = arr("L0_rec_W0").reshape(FIELDS, FIELDS, LAYER)
    pairs = [np.zeros((FIELDS, DELTAS, K0, LAYER), w.dtype) for _ in range(2)]
    fields = np.arange(FIELDS)
    for k in range(K0):
        for j in range(DELTAS):
            delta = k * DELTAS + j
            if delta < OFFSETS:
                pairs[0][:, j, k] = w[fields, (fields + delta) % FIELDS]
                if delta > 0:
                    pairs[1][:, j, k] = w[(fields + delta) % FIELDS, fields]
    w0a = given("w0a_in", pairs[0].reshape(ROWS0, K0, LAYER))
    w0b = given("w0b_in", pairs[1].reshape(ROWS0, K0 * LAYER))

    def by_tile(w):
        full = np.zeros((KF * FQ, HIDDEN, LAYER), w.dtype)
        full[:FIELDS] = w.reshape(FIELDS, HIDDEN, LAYER)
        return full.reshape(KF, FQ, NG, GB, LAYER).transpose(1, 3, 2, 0, 4).reshape(P, SL, PAIR * LAYER)

    w12 = np.stack([by_tile(arr("L0_rec_W1")), by_tile(arr("L0_rec_W2"))], axis=1)
    w_whole = given("w_whole_in", w12[:, :, list(WHOLE)].reshape(P, -1))
    w_split = given("w_split_in", w12[:, :, list(SPLIT)].reshape(P, -1))
    b_cin = given("b_cin_in", np.stack([arr(f"L0_rec_b{i}") for i in range(3)], axis=1))
    wt1 = given("wt1_in", arr("W_top1"))
    bt1 = given("bt1_in", arr("b_top1").reshape(M1, P).T)
    wt2 = given("wt2_in", arr("W_top2"))
    bt2 = given("bt2_in", arr("b_top2").reshape(M2, P).T)
    wt3 = given("wt3_in", arr("W_top3").reshape(M2, P).T)
    y = nc.dram_tensor("y_out", (1, BATCH), F32, kind="ExternalOutput").ap()

    build(nc, ids, tables, dense_t, w0a, w0b, w_whole, w_split, b_cin, wt1, bt1, wt2, bt2, wt3, y)
    result = run_bass_kernel_spmd(nc, [arrays], core_ids=[0])
    return result.results[0]["y_out"].reshape(BATCH, 1)
```

```python
from contextlib import ExitStack

import numpy as np
import concourse.bass as bass
from concourse import mybir

F32 = mybir.dt.float32
F32R = mybir.dt.float32r
I32 = mybir.dt.int32
ALU = mybir.AluOpType
ACT = mybir.ActivationFunctionType
AX = mybir.AxisListType

P = 128
BATCH = 2048
FIELDS = 39
DIM = 16
TILES = BATCH // P
DB = 4
BPT = DIM // DB
BLOCKS = TILES * BPT
COLS = DB * P
LAYER = 128
HIDDEN = LAYER // 2
DELTAS = 3
OFFSETS = FIELDS // 2 + 1
K0 = -(-OFFSETS // DELTAS)
ROWS0 = FIELDS * DELTAS
FQ = 4
GB = 32
KF = -(-FIELDS // FQ)
NG = HIDDEN // GB
XROWS = FIELDS + K0 * DELTAS - 1
PAIR = 2
SG = KF // PAIR
KINDS = ("F" * -(-K0 // PAIR), "PNDPDPPNPN", "PNDPDPPNNN")
SLOTS = tuple(len(k) for k in KINDS)
WHOLE_W = [(layer, i) for layer in (1, 2) for i in range(SLOTS[layer]) if KINDS[layer][i] == "N"]
SPLIT_W = [(layer, i) for layer in (1, 2) for i in range(SLOTS[layer]) if KINDS[layer][i] != "N"]
N_RING = 4
RAW_RING = 2
P_RING = 4
D_RING = 4
GATHERS = (12, 12, 11, 4)
FIRST_GATHERS = 31
SCR = 4
XC = 2
READ0_AFTER, READ1_AFTER = (7, 9, 9), (7, 9, 9)
READ2_AFTER = 3
READ_X_AFTER = 5
EMB_AFTER = 5
SUM01_AFTER = 5
FIRST_AFTER = (5, 6, 8, 9)
assert all(KINDS[1][i] != "D" for i in (*READ0_AFTER, READ2_AFTER, READ_X_AFTER, SUM01_AFTER))
assert all(KINDS[2][i] != "D" for i in (*READ1_AFTER, READ2_AFTER, EMB_AFTER, *FIRST_AFTER))
DENSE = 16
H1, H2 = 512, 256
M1, M2 = H1 // P, H2 // P
CHUNKS = BATCH // COLS
assert SLOTS[1] == SLOTS[2] == NG * SG and KF % PAIR == 0 and BPT == 4 and SCR == BPT
assert sum(GATHERS) == FIELDS


def slots_before(kinds, layer, m, i=0):
    s1, s2 = (sum(k in kinds for k in KINDS[n]) for n in (1, 2))
    within = sum(k in kinds for k in KINDS[layer][:i])
    peeled = isinstance(m, int)
    last = s1 + (s1 + s2) * (BLOCKS - 2)
    if layer == 1:
        if peeled and m in (0, BLOCKS - 1):
            return (0 if m == 0 else last) + within
        return m * (s1 + s2) + (within - s2)
    if peeled and m >= BLOCKS - 2:
        return last + s1 + (m - (BLOCKS - 2)) * s2 + within
    return m * (s1 + s2) + (2 * s1 + within)


for _kinds, _ring, _size in (("N", N_RING, 1), ("P", RAW_RING, 1), ("P", P_RING, 1), ("D", D_RING, PAIR)):
    assert BPT * _size * sum(k in _kinds for ks in KINDS[1:] for k in ks) % _ring == 0


def vector_order(layer):
    tiles = [(i, k) for i in range(SLOTS[layer]) if KINDS[layer][i] == "D" for k in range(PAIR)]
    order, open_tile = [], None
    for i in range(SLOTS[layer]):
        if KINDS[layer][i] == "D":
            continue
        order.append(("slot", i))
        if open_tile:
            order.append(("rest", *open_tile))
            open_tile = None
        if tiles and tiles[0][0] <= i + 1:
            open_tile = tiles.pop(0)
            order.append(("mult", *open_tile))
    if open_tile:
        order.append(("rest", *open_tile))
    assert not tiles and order[-1] == ("slot", SLOTS[layer] - 1)
    return order


def group_index(layer, m):
    peeled = isinstance(m, int)
    if layer == 0:
        return m if peeled and m < 2 else m * 3 - 3
    if layer == 1:
        if peeled and m == 0:
            return 2
        return 3 * m if peeled and m == BLOCKS - 1 else m * 3 + 1
    if peeled and m >= BLOCKS - 2:
        return 3 * (BLOCKS - 1) + 1 + (m - (BLOCKS - 2))
    return m * 3 + 5


def build(nc, ids, tables, dense_t, w0a, w0b, w_whole, w_split, b_cin, wt1, bt1, wt2, bt2, wt3, y):
    with ExitStack() as ctx:
        def sb(name, shape, dt=F32):
            return ctx.enter_context(nc.sbuf_tensor(name, shape, dt))

        def ps(name, shape):
            return ctx.enter_context(nc.psum_tensor(name, shape, F32))

        def sem(name):
            return ctx.enter_context(nc.semaphore(name))

        x_scratch = nc.dram_tensor("x_scratch", (SCR, XROWS, COLS), F32)
        z_scratch = nc.dram_tensor("z_scratch", (2, P, BATCH), F32)

        ids_tile = sb("ids_tile", [P, FIELDS], I32)
        emb = sb("emb", [P, FIELDS * DIM])
        emb_rep = sb("emb_rep", [P, DIM, ROWS0])
        ident = sb("ident", [P, P])
        x_t = sb("x_t", [ROWS0, COLS])
        x_shift = sb("x_shift", [P, K0, COLS])
        x_copy = sb("x_copy", [P, XC, KF, COLS])
        prod = sb("prod", [P, SLOTS[0] + N_RING + RAW_RING, PAIR, COLS])
        p_hi = sb("p_hi", [P, P_RING, PAIR, COLS], F32R)
        p_lo = sb("p_lo", [P, P_RING, PAIR, COLS], F32R)
        d_hi = sb("d_hi", [P, D_RING, COLS], F32R)
        d_lo = sb("d_lo", [P, D_RING, COLS], F32R)
        w0_sb = sb("w0_sb", [ROWS0, K0, LAYER])
        w_sb = sb("w_sb", [P, len(WHOLE_W), PAIR, LAYER])
        w_hi = sb("w_hi", [P, len(SPLIT_W), PAIR, LAYER], F32R)
        w_lo = sb("w_lo", [P, len(SPLIT_W), PAIR, LAYER], F32R)
        w_staged = x_copy[:, 1, :, :].rearrange("p k c -> p (k c)")[:, 0:len(SPLIT_W) * PAIR * LAYER]
        b_sb = sb("b_sb", [P, 3])
        direct01 = sb("direct01", [P, 2, COLS])
        direct2 = sb("direct2", [P, COLS])
        part01 = sb("part01", [P, BPT, P])
        part2 = sb("part2", [P, BPT, P])
        z01 = sb("z01", [P, P])
        z2 = sb("z2", [P, P])
        bt1_sb = sb("bt1_sb", [P, M1])
        bt2_sb = sb("bt2_sb", [P, M2])
        wt3_sb = sb("wt3_sb", [P, M2])
        z_all = x_copy[:, 0, 0:2 * CHUNKS, :].rearrange("p (k c) n -> p k c n", k=2)
        h1 = x_copy[:, 1, 0:2 * M1, :].rearrange("p (a m) n -> p a m n", a=2)
        h2 = prod[:, 0:2, :, :]
        y_sb = prod[0:1, 2:4, :, :].rearrange("p a b n -> p (a b) n")
        shift_flat = x_shift[:, :, :].rearrange("p k n -> p (k n)")
        wt1_z = shift_flat[:, 0:2 * H1].rearrange("p (k n) -> p k n", k=2)
        wt1_d = shift_flat[0:DENSE, 2 * H1:3 * H1]
        dense_sb = shift_flat[0:DENSE, 3 * H1:3 * H1 + BATCH]
        wt2_sb = emb_rep[:, :, :].rearrange("p d f -> p (d f)")[:, 0:M1 * H2].rearrange("p (k n) -> p k n", k=M1)

        x_rep = ps("x_rep", [ROWS0, COLS])
        hid = [ps(f"hid{layer}", [P, NG, COLS]) for layer in (1, 2)]
        acc = ps("acc", [P, 2, COLS])
        stage = ps("stage", [P, COLS])

        ids_loaded = sem("ids_loaded")
        w_loaded = sem("w_loaded")
        mlp_w_loaded = sem("mlp_w_loaded")
        w0_summed = sem("w0_summed")
        w_rounded = sem("w_rounded")
        w_parted = sem("w_parted")
        ident_zeroed = sem("ident_zeroed")
        ident_ready = sem("ident_ready")
        gathers_begun = sem("gathers_begun")
        gathered = sem("gathered")
        emb_copied = sem("emb_copied")
        transposed = sem("transposed")
        x_t_ready = sem("x_t_ready")
        scratch_written = sem("scratch_written")
        shift_loaded = sem("shift_loaded")
        copy_loaded = [sem(f"copy_loaded{i}") for i in range(SG)]
        first_ready = sem("first_ready")
        first_used = sem("first_used")
        prod_ready = sem("prod_ready")
        whole_used = sem("whole_used")
        hi_ready = sem("hi_ready")
        lo_ready = sem("lo_ready")
        split_used = sem("split_used")
        tile_staged = sem("tile_staged")
        tile_hi = sem("tile_hi")
        tile_lo = sem("tile_lo")
        tile_used = sem("tile_used")
        group_read = sem("group_read")
        hidden_ready = [sem(f"hidden_ready{layer}") for layer in (1, 2)]
        reduced = sem("reduced")
        parts01 = sem("parts01")
        parts2 = sem("parts2")
        z01_ready = sem("z01_ready")
        z2_ready = sem("z2_ready")
        z_written = sem("z_written")
        z_loaded = sem("z_loaded")
        last_z_loaded = sem("last_z_loaded")
        mlp1_done = sem("mlp1_done")
        mlp2_done = sem("mlp2_done")
        mlp3_done = sem("mlp3_done")
        h1_ready = sem("h1_ready")
        h2_ready = sem("h2_ready")
        y_ready = sem("y_ready")
        y_written = sem("y_written")

        block = ctx.enter_context(nc.Block())

        def prod_at(layer, r, i):
            if layer == 0:
                return i
            if KINDS[layer][i] == "N":
                return SLOTS[0] + slots_before("N", layer, r, i) % N_RING
            return SLOTS[0] + N_RING + slots_before("P", layer, r, i) % RAW_RING

        def wait_multiplied(eng, layer, m, slot):
            if layer == 0:
                eng.wait_ge(first_ready, m * SLOTS[0] + (slot + 1))
            elif KINDS[layer][slot] == "D":
                eng.wait_ge(tile_staged, slots_before("D", layer, m, slot + 1) * PAIR)
            else:
                eng.wait_ge(prod_ready, slots_before("NP", layer, m, slot + 1))

        def wait_contracted(eng, layer, m, slot):
            kind = KINDS[layer][slot]
            if kind == "F":
                eng.wait_ge(first_used, m * SLOTS[0] + (slot + 1))
                return
            before = slots_before(kind, layer, m, slot + 1)
            if kind == "D":
                eng.wait_ge(tile_used, before * PAIR)
            else:
                eng.wait_ge(split_used if kind == "P" else whole_used, before)

        def steps(eng, body):
            for r in range(BPT):
                body(r, r)
            with eng.Fori(1, TILES - 1) as t:
                for j in range(BPT):
                    body(t * BPT + j, 2 * BPT + j)
            for r in range(BLOCKS - BPT, BLOCKS):
                body(r, r)

        @block.sync
        def _(sp):
            def load_ids(t):
                if isinstance(t, int):
                    first = t * FIELDS
                else:
                    first = sp.snap(t * FIELDS)
                if not (isinstance(t, int) and t == 0):
                    sp.wait_ge(gathered, t * (16 * FIELDS))
                sp.dma_start(ids_tile[:, :], ids[:, bass.ds(first, FIELDS)]).then_inc(ids_loaded, 16)

            load_ids(0)
            sp.dma_start(w0_sb[:, :, :], w0a).then_inc(w_loaded, 16)
            sp.dma_start(prod[0:ROWS0, 0:2, :, :].rearrange("p a b c -> p (a b c)")[:, 0:K0 * LAYER],
                         w0b).then_inc(w_loaded, 16)
            sp.dma_start(b_sb[:, :], b_cin).then_inc(w_loaded, 16)
            sp.dma_start(w_staged, w_split).then_inc(w_loaded, 16)
            sp.dma_start(w_sb[:, :, :, :].rearrange("p a b c -> p (a b c)"), w_whole).then_inc(w_loaded, 16)
            sp.dma_start(bt1_sb[:, :], bt1).then_inc(mlp_w_loaded, 16)
            sp.dma_start(bt2_sb[:, :], bt2).then_inc(mlp_w_loaded, 16)
            sp.dma_start(wt3_sb[:, :], wt3).then_inc(mlp_w_loaded, 16)

            def load_shift(m, r):
                slot = r % SCR
                sp.wait_ge(x_t_ready, m + 1)
                sp.dma_start(x_scratch.ap()[slot, 0:FIELDS, :],
                             x_t[0:ROWS0:DELTAS, :]).then_inc(scratch_written, 16)
                sp.dma_start(x_scratch.ap()[slot, FIELDS:XROWS, :],
                             x_t[0:(XROWS - FIELDS) * DELTAS:DELTAS, :]).then_inc(scratch_written, 16)
                sp.wait_ge(scratch_written, m * 32 + 32)
                if r >= 1:
                    wait_multiplied(sp, 0, m - 1, SLOTS[0] - 1)
                for k in range(K0):
                    src = bass.AP(tensor=x_scratch, offset=(slot * XROWS + k * DELTAS) * COLS,
                                  ap=[[COLS, FIELDS], [COLS, DELTAS], [1, COLS]])
                    sp.dma_start(x_shift[0:ROWS0, k, :], src).then_inc(shift_loaded, 16)

            def load_copies(m, r):
                if r == 1:
                    sp.wait_ge(w_parted, 1)
                for i in range(SG):
                    if r == 1:
                        wait_multiplied(sp, 1, 0, i)
                    if r >= XC:
                        wait_multiplied(sp, 2, m - XC, SLOTS[2] - SG + i)
                    for q in range(FQ):
                        src = bass.AP(tensor=x_scratch, offset=((r % SCR) * XROWS + i * PAIR * FQ + q) * COLS,
                                      ap=[[0, GB], [FQ * COLS, PAIR], [1, COLS]])
                        sp.dma_start(x_copy[q * GB:(q + 1) * GB, r % XC, i * PAIR:(i + 1) * PAIR, :],
                                     src).then_inc(copy_loaded[i], 16)

            def write_z(t):
                first = t * P if isinstance(t, int) else sp.snap(t * P)
                sp.wait_ge(z01_ready, t + 1)
                sp.wait_ge(z2_ready, t + 1)
                for k, z in enumerate((z01, z2)):
                    sp.dma_start(z_scratch.ap()[k, :, bass.ds(first, P)], z[:, :]).then_inc(z_written, 16)

            load_ids(1)
            load_shift(0, 0)
            load_shift(1, 1)
            load_copies(0, 0)

            def step(n, r, t):
                if r % BPT == 2 and r < BLOCKS - 2 * BPT:
                    load_ids(t + 2)
                if r < BLOCKS - 2:
                    load_shift(n + 2, r + 2)
                if r < BLOCKS - 1:
                    load_copies(n + 1, r + 1)
                if r >= BPT and r % BPT == 2:
                    write_z(t - 1)

            for r in range(BPT):
                step(r, r, 0)
            with sp.Fori(1, TILES - 2) as t:
                for j in range(BPT):
                    step(t * BPT + j, 2 * BPT + j, t)
            for r in range(BLOCKS - 2 * BPT, BLOCKS):
                step(r, r, r // BPT)

            wait_multiplied(sp, 0, BLOCKS - 1, SLOTS[0] - 1)
            sp.wait_ge(transposed, BLOCKS)
            sp.dma_start(wt1_z, wt1[0:2 * P, :].rearrange("(k p) n -> p k n", p=P)).then_inc(mlp_w_loaded, 16)
            sp.dma_start(wt1_d, wt1[2 * P:2 * P + DENSE, :]).then_inc(mlp_w_loaded, 16)
            sp.dma_start(wt2_sb, wt2.rearrange("(k p) n -> p k n", p=P)).then_inc(mlp_w_loaded, 16)
            sp.dma_start(dense_sb, dense_t).then_inc(mlp_w_loaded, 16)
            for i in range(SLOTS[2]):
                wait_multiplied(sp, 2, BLOCKS - 2, i)
            sp.wait_ge(z_written, 32 * (TILES - 1))
            done = (CHUNKS - 1) * COLS
            for k in range(2):
                sp.dma_start(z_all[:, k, 0:CHUNKS - 1, :], z_scratch.ap()[k, :, 0:done]).then_inc(z_loaded, 16)
            write_z(TILES - 1)
            sp.wait_ge(z_written, 32 * TILES)
            for k in range(2):
                sp.dma_start(z_all[:, k, CHUNKS - 1, :], z_scratch.ap()[k, :, done:BATCH]).then_inc(last_z_loaded, 16)
            sp.wait_ge(scratch_written, 32 * BLOCKS)

        @block.gpsimd
        def _(pool):
            nc.gpsimd.memset(ident[:, :], 0.0).then_inc(ident_zeroed, 1)

            def begin_gathers(t):
                pool.wait_ge(ids_loaded, (t + 1) * 16)
                if not (isinstance(t, int) and t == 0):
                    pool.wait_ge(emb_copied, t)
                pool.sem_inc(gathers_begun, 1)

            def gather(f):
                nc.gpsimd.indirect_dma_start(
                    out=emb[:, f * DIM:(f + 1) * DIM], out_offset=None, in_=tables[f],
                    in_offset=bass.IndirectOffsetOnAxis(ap=ids_tile[:, f:f + 1], axis=0),
                ).then_inc(gathered, 16)

            def part_slot(layer, m, r, i):
                pos = prod_at(layer, r, i)
                at = slots_before("P", layer, r, i) % P_RING
                pool.wait_ge(hi_ready, slots_before("P", layer, m, i + 1))
                nc.gpsimd.tensor_tensor(p_lo[:, at, :, :], prod[:, pos, :, :],
                                        p_hi[:, at, :, :].bitcast(F32), ALU.subtract).then_inc(lo_ready, 1)

            p_slots = [[i for i in range(SLOTS[layer]) if KINDS[layer][i] == "P"] for layer in range(3)]

            def step(n, r, t):
                if r < 2:
                    todo = list(range(FIRST_GATHERS + r, FIELDS, 2))
                elif r < BLOCKS - BPT - 2:
                    f = sum(GATHERS[:(r - 2) % BPT])
                    todo = list(range(f, f + GATHERS[(r - 2) % BPT]))
                else:
                    todo = []
                work = [(1, n, r, i) for i in p_slots[1]]
                if r >= 1:
                    work += [(2, n - 1, r - 1, i) for i in p_slots[2]]
                for i, w in enumerate(work):
                    part_slot(*w)
                    if i == 1 and todo and r % BPT == 2:
                        begin_gathers(t + 2)
                    if i >= 2 and todo:
                        gather(todo.pop(0))
                for f in todo:
                    gather(f)

            begin_gathers(0)
            for f in range(FIELDS):
                gather(f)
            pool.wait_ge(ident_zeroed, 1)
            nc.gpsimd.affine_select(out=ident[:, :], in_=ident[:, :], compare_op=ALU.not_equal, fill=1.0,
                                    base=0, pattern=[[-1, P]], channel_multiplier=1).then_inc(ident_ready, 1)
            begin_gathers(1)
            for f in range(FIRST_GATHERS):
                gather(f)
            for r in range(BPT):
                step(r, r, 0)
            with pool.Fori(1, TILES - 2) as t:
                for j in range(BPT):
                    step(t * BPT + j, 2 * BPT + j, t)
            for r in range(BLOCKS - 2 * BPT, BLOCKS):
                step(r, r, r // BPT)
            for i in p_slots[2]:
                part_slot(2, BLOCKS - 1, BLOCKS - 1, i)

        @block.scalar
        def _(act):
            def copy_emb(t):
                act.wait_ge(gathered, (t + 1) * (16 * FIELDS))
                if not (isinstance(t, int) and t == 0):
                    act.wait_ge(transposed, t * BPT)
                src = emb[:, :].rearrange("p (f d) -> p d f", d=DIM).unsqueeze(3).to_broadcast([P, DIM, FIELDS, DELTAS])
                dst = emb_rep[:, :, :].rearrange("p d (f j) -> p d f j", j=DELTAS)
                nc.scalar.activation(dst, src, ACT.Copy).then_inc(emb_copied, 1)

            def read_x(m, r):
                act.wait_ge(transposed, m + 1)
                if r >= 1:
                    act.wait_ge(scratch_written, m * 32)
                nc.scalar.activation(x_t[:, :], x_rep[:, :], ACT.Copy).then_inc(x_t_ready, 1)

            def read_hidden(layer, m, r, g):
                wait_contracted(act, layer, m, SLOTS[layer] - 1)
                if r >= 1:
                    slots = range(g * SG, (g + 1) * SG)
                    last_d = [i for i in slots if KINDS[layer + 1][i] == "D"][-1:]
                    for i in sorted({slots[-1], *last_d}):
                        wait_multiplied(act, layer + 1, m - 1, i)
                for q in range(FQ):
                    last = nc.scalar.activation(
                        hid[layer][q * GB:(q + 1) * GB, g, :],
                        acc[g * GB:(g + 1) * GB, group_index(layer, r) % 2, :], ACT.Relu,
                        bias=b_sb[g * GB:(g + 1) * GB, layer:layer + 1])
                last.then_inc(hidden_ready[layer], 1)

            def read_direct(layer, m, r):
                wait_contracted(act, layer, m, SLOTS[layer] - 1)
                bank = acc[:, group_index(layer, r) % 2, :]
                if layer < 2:
                    if layer == 0 and r >= 2:
                        act.wait_ge(reduced, m - 1)
                    nc.scalar.activation(direct01[layer * HIDDEN:(layer + 1) * HIDDEN, r % 2, :],
                                         bank[HIDDEN:LAYER, :], ACT.Relu,
                                         bias=b_sb[HIDDEN:LAYER, layer:layer + 1]).then_inc(group_read, 1)
                else:
                    if r >= 1:
                        act.wait_ge(parts2, m)
                    nc.scalar.activation(direct2[:, :], bank, ACT.Relu,
                                         bias=b_sb[:, layer:layer + 1]).then_inc(group_read, 1)

            def round_slot(layer, m, r, i):
                pos = prod_at(layer, r, i)
                index = slots_before("P", layer, r, i)
                act.wait_ge(prod_ready, slots_before("NP", layer, m, i + 1))
                if index >= P_RING:
                    act.wait_ge(split_used, slots_before("P", layer, m, i) + (1 - P_RING))
                nc.scalar.activation(p_hi[:, index % P_RING, :, :], prod[:, pos, :, :], ACT.Copy).then_inc(hi_ready, 1)

            def round_tile(layer, m, r, i, k):
                index = slots_before("D", layer, r, i) * PAIR + k
                act.wait_ge(tile_staged, slots_before("D", layer, m, i) * PAIR + (k + 1))
                if index >= D_RING:
                    act.wait_ge(tile_used, slots_before("D", layer, m, i) * PAIR + (k + 1 - D_RING))
                nc.scalar.activation(d_hi[:, index % D_RING, :], stage[:, :], ACT.Copy).then_inc(tile_hi, 1)

            def round_layer(layer, m, r, after_slot):
                for what, i, *k in vector_order(layer):
                    if what == "slot" and KINDS[layer][i] == "P":
                        round_slot(layer, m, r, i)
                    if what == "mult":
                        round_tile(layer, m, r, i, *k)
                    if what == "slot":
                        after_slot(i)

            act.wait_ge(w_loaded, 16 * 5)
            nc.scalar.activation(w_hi[:, :, :, :].rearrange("p a b c -> p (a b c)"), w_staged,
                                 ACT.Copy).then_inc(w_rounded, 1)
            copy_emb(0)
            read_x(0, 0)
            read_x(1, 1)
            read_hidden(0, 0, 0, 0)
            read_hidden(0, 0, 0, 1)
            read_direct(0, 0, 0)

            def step(n, r, t):
                def after_slot_of_layer1(i):
                    if i == READ2_AFTER and r >= 2:
                        read_direct(2, n - 2, r - 2)
                    if i == READ_X_AFTER and r < BLOCKS - 2:
                        read_x(n + 2, r + 2)
                    for part in range(NG + 1):
                        if i == READ0_AFTER[part] and r < BLOCKS - 1:
                            if part < NG:
                                read_hidden(0, n + 1, r + 1, part)
                            else:
                                read_direct(0, n + 1, r + 1)

                def after_slot_of_layer2(i):
                    if i == EMB_AFTER and r % BPT == 1 and r < BLOCKS - BPT:
                        copy_emb(t + 1)
                    for part in range(NG + 1):
                        if i == READ1_AFTER[part]:
                            if part < NG:
                                read_hidden(1, n, r, part)
                            else:
                                read_direct(1, n, r)

                round_layer(1, n, r, after_slot_of_layer1)
                if r >= 1:
                    round_layer(2, n - 1, r - 1, after_slot_of_layer2)
                else:
                    for i in range(SLOTS[2]):
                        after_slot_of_layer2(i)

            for r in range(BPT):
                step(r, r, 0)
            with act.Fori(1, TILES - 1) as t:
                for j in range(BPT):
                    step(t * BPT + j, 2 * BPT + j, t)
            for r in range(BLOCKS - BPT, BLOCKS):
                step(r, r, TILES - 1)

            def after_last_slots(i):
                if i == READ2_AFTER:
                    read_direct(2, BLOCKS - 2, BLOCKS - 2)

            round_layer(2, BLOCKS - 1, BLOCKS - 1, after_last_slots)
            read_direct(2, BLOCKS - 1, BLOCKS - 1)

            act.wait_ge(mlp_w_loaded, 16 * 7)

            def read_h1(c):
                for i in range(0, M1, 2):
                    act.wait_ge(mlp1_done, M1 * c + i + 1)
                    if c >= 2:
                        act.wait_ge(mlp2_done, M2 * (c - 1))
                    nc.scalar.activation(h1[:, c % 2, i, :], hid[i // NG][:, i % NG, :], ACT.Relu,
                                         bias=bt1_sb[:, i:i + 1]).then_inc(h1_ready, 1)

            def read_h2(c):
                act.wait_ge(mlp2_done, M2 * c + 1)
                if c >= 2:
                    act.wait_ge(mlp3_done, c - 1)
                nc.scalar.activation(h2[:, c % 2, 0, :], acc[:, 0, :], ACT.Relu,
                                     bias=bt2_sb[:, 0:1]).then_inc(h2_ready, 1)

            def write_y(c):
                act.wait_ge(mlp3_done, c + 1)
                nc.scalar.activation(y_sb[:, c, :], stage[0:1, :], ACT.Copy).then_inc(y_ready, 1)
                act.wait_ge(y_ready, c + 1)
                act.dma_start(y[:, c * COLS:(c + 1) * COLS], y_sb[:, c, :]).then_inc(y_written, 16)

            read_h1(0)
            for c in range(CHUNKS):
                if c + 1 < CHUNKS:
                    read_h1(c + 1)
                read_h2(c)
                if c >= 1:
                    write_y(c - 1)
            write_y(CHUNKS - 1)
            act.wait_ge(y_written, 16 * CHUNKS)

        @block.vector
        def _(dve):
            dve.wait_ge(w_loaded, 16 * 5)
            nc.vector.tensor_tensor(
                w0_sb[:, :, :], w0_sb[:, :, :],
                prod[0:ROWS0, 0:2, :, :].rearrange("p a b c -> p (a b c)")[:, 0:K0 * LAYER]
                .rearrange("p (k s) -> p k s", k=K0), ALU.add).then_inc(w0_summed, 1)
            dve.wait_ge(w_rounded, 1)
            nc.vector.tensor_tensor(
                w_lo[:, :, :, :].rearrange("p a b c -> p (a b c)"), w_staged,
                w_hi[:, :, :, :].rearrange("p a b c -> p (a b c)").bitcast(F32),
                ALU.subtract).then_inc(w_parted, 1)
            dve.wait_ge(w0_summed, 1)

            def free_slot(layer, m, r, i):
                kind = KINDS[layer][i]
                ring = N_RING if kind == "N" else RAW_RING
                if slots_before(kind, layer, r, i) >= ring:
                    dve.wait_ge(whole_used if kind == "N" else lo_ready,
                                slots_before(kind, layer, m, i) + (1 - ring))
                return prod_at(layer, r, i)

            def products0(m, r, i):
                if i == 0:
                    dve.wait_ge(shift_loaded, (m + 1) * (16 * K0))
                    dve.wait_ge(transposed, m + 1)
                if r >= 1:
                    dve.wait_ge(first_used, m * SLOTS[0] + (i + 1 - SLOTS[0]))
                k, n = i * PAIR, min(PAIR, K0 - i * PAIR)
                nc.vector.tensor_tensor(
                    prod[0:ROWS0, i, 0:n, :],
                    x_rep[:, :].unsqueeze(1).to_broadcast([ROWS0, n, COLS]),
                    x_shift[0:ROWS0, k:k + n, :], ALU.mult).then_inc(first_ready, 1)

            def products(layer, m, r, after_slot):
                for n, (what, i, *tile) in enumerate(vector_order(layer)):
                    g, pair = divmod(i, SG)
                    index = slots_before("D", layer, r, i) * PAIR + sum(tile)
                    count = slots_before("D", layer, m, i) * PAIR + sum(tile)
                    if what != "rest":
                        if g == 0 and not sum(tile):
                            dve.wait_ge(copy_loaded[pair], (m + 1) * (16 * FQ))
                        if n == 0 or i == SG:
                            dve.wait_ge(hidden_ready[layer - 1], m * NG + (g + 1))
                    left = hid[layer - 1][:, g, :]
                    if what == "slot":
                        slot = free_slot(layer, m, r, i)
                        nc.vector.tensor_tensor(
                            prod[:, slot, :, :], left.unsqueeze(1).to_broadcast([P, PAIR, COLS]),
                            x_copy[:, r % XC, pair * PAIR:(pair + 1) * PAIR, :], ALU.mult).then_inc(prod_ready, 1)
                    if what == "mult":
                        if index >= 1:
                            dve.wait_ge(tile_lo, count)
                        nc.vector.tensor_tensor(stage[:, :], left, x_copy[:, r % XC, pair * PAIR + tile[0], :],
                                                ALU.mult).then_inc(tile_staged, 1)
                    if what == "rest":
                        dve.wait_ge(tile_hi, count + 1)
                        nc.vector.tensor_tensor(d_lo[:, index % D_RING, :], stage[:, :],
                                                d_hi[:, index % D_RING, :].bitcast(F32),
                                                ALU.subtract).then_inc(tile_lo, 1)
                    if what == "slot":
                        after_slot(i)

            def sum_block(direct, part, slot):
                return nc.vector.tensor_reduce(
                    part[:, slot, :], direct.rearrange("p (d b) -> p b d", d=DB), AX.X, ALU.add)

            def sum_tile(part, z):
                return nc.vector.tensor_reduce(z[:, :], part[:, :, :].rearrange("p j b -> p b j"), AX.X, ALU.add)

            def sum01(m, r, t):
                dve.wait_ge(group_read, group_index(1, m) + 1)
                if r >= BPT and r % BPT == 0:
                    dve.wait_ge(z01_ready, t)
                sum_block(direct01[:, r % 2, :], part01, r % BPT).then_inc(reduced, 1)
                if r % BPT == BPT - 1:
                    dve.wait_ge(reduced, m + 1)
                    if r >= BPT:
                        dve.wait_ge(z_written, t * 32)
                    sum_tile(part01, z01).then_inc(z01_ready, 1)

            def sum2(m, r, t):
                dve.wait_ge(group_read, group_index(2, m) + 1)
                if r >= BPT and r % BPT == 0:
                    dve.wait_ge(z2_ready, t)
                sum_block(direct2[:, :], part2, r % BPT).then_inc(parts2, 1)
                if r % BPT == BPT - 1:
                    dve.wait_ge(parts2, m + 1)
                    if r >= BPT:
                        dve.wait_ge(z_written, t * 32)
                    sum_tile(part2, z2).then_inc(z2_ready, 1)

            for m in range(2):
                for i in range(SLOTS[0]):
                    products0(m, m, i)

            def step(n, r, t):
                def after_slot_of_layer1(i):
                    if i == SUM01_AFTER and r >= 1:
                        sum01(n - 1, r - 1, t if r % BPT >= 1 else t - 1)

                def after_slot_of_layer2(i):
                    for first in range(SLOTS[0]):
                        if i == FIRST_AFTER[first] and r < BLOCKS - 2:
                            products0(n + 2, r + 2, first)

                products(1, n, r, after_slot_of_layer1)
                if r >= 2:
                    sum2(n - 2, r - 2, t if r % BPT >= 2 else t - 1)
                if r >= 1:
                    products(2, n - 1, r - 1, after_slot_of_layer2)
                else:
                    for i in range(SLOTS[2]):
                        after_slot_of_layer2(i)

            for r in range(BPT):
                step(r, r, 0)
            with dve.Fori(1, TILES - 1) as t:
                for j in range(BPT):
                    step(t * BPT + j, 2 * BPT + j, t)
            for r in range(BLOCKS - BPT, BLOCKS):
                step(r, r, TILES - 1)
            products(2, BLOCKS - 1, BLOCKS - 1, lambda i: None)
            sum2(BLOCKS - 2, BLOCKS - 2, TILES - 1)
            sum01(BLOCKS - 1, BLOCKS - 1, TILES - 1)
            sum2(BLOCKS - 1, BLOCKS - 1, TILES - 1)

            dve.wait_ge(mlp_w_loaded, 16 * 7)

            def bias_relu(out, bank, bias):
                return nc.vector.tensor_scalar(out, bank, bias, 0.0, ALU.add, ALU.max)

            def read_h1(c):
                for i in range(1, M1, 2):
                    dve.wait_ge(mlp1_done, M1 * c + i + 1)
                    if c >= 2:
                        dve.wait_ge(mlp2_done, M2 * (c - 1))
                    bias_relu(h1[:, c % 2, i, :], hid[i // NG][:, i % NG, :],
                              bt1_sb[:, i:i + 1]).then_inc(h1_ready, 1)

            read_h1(0)
            for c in range(CHUNKS):
                if c + 1 < CHUNKS:
                    read_h1(c + 1)
                dve.wait_ge(mlp2_done, M2 * (c + 1))
                if c >= 2:
                    dve.wait_ge(mlp3_done, c - 1)
                bias_relu(h2[:, c % 2, 1, :], acc[:, 1, :], bt2_sb[:, 1:2]).then_inc(h2_ready, 1)

        @block.tensor
        def _(pe):
            def transpose_block(m, r, t):
                pe.wait_ge(emb_copied, t + 1)
                if r >= 1:
                    wait_multiplied(pe, 0, m - 1, SLOTS[0] - 1)
                    pe.wait_ge(x_t_ready, m)
                for d in range(DB):
                    last = nc.tensor.transpose(x_rep[:, d * P:(d + 1) * P], emb_rep[:, (r % BPT) * DB + d, :],
                                               ident[:, :])
                last.then_inc(transposed, 1)

            def contract(layer, m, r):
                bank = acc[:, group_index(layer, r) % 2, :]
                if group_index(layer, r) >= 2:
                    pe.wait_ge(group_read, group_index(layer, m) - 1)
                def product(w, rhs, first=False, last=False):
                    return nc.tensor.matmul(bank, w, rhs, start=first, stop=last)

                order = [item for item in vector_order(layer) if item[0] != "mult"]
                for n, (_, i, *tile) in enumerate(order):
                    kind = KINDS[layer][i]
                    start, stop = n == 0, n == len(order) - 1
                    if kind in "FN":
                        wait_multiplied(pe, layer, m, i)
                        slot = prod_at(layer, r, i)
                        tiles = min(PAIR, K0 - i * PAIR) if layer == 0 else PAIR
                        for k in range(tiles):
                            if layer == 0:
                                w, rhs = w0_sb[:, i * PAIR + k, :], prod[0:ROWS0, slot, k, :]
                            else:
                                w, rhs = w_sb[:, WHOLE_W.index((layer, i)), k, :], prod[:, slot, k, :]
                            last = product(w, rhs, start and k == 0, stop and k == tiles - 1)
                        last.then_inc(whole_used if kind == "N" else first_used, 1)
                    if kind == "P":
                        e = SPLIT_W.index((layer, i))
                        at = slots_before("P", layer, r, i) % P_RING
                        pe.wait_ge(hi_ready, slots_before("P", layer, m, i + 1))
                        for k in range(PAIR):
                            product(w_hi[:, e, k, :], p_hi[:, at, k, :], start and k == 0)
                            product(w_lo[:, e, k, :], p_hi[:, at, k, :])
                        pe.wait_ge(lo_ready, slots_before("P", layer, m, i + 1))
                        for k in range(PAIR):
                            last = product(w_hi[:, e, k, :], p_lo[:, at, k, :], False, stop and k == PAIR - 1)
                        last.then_inc(split_used, 1)
                    if kind == "D":
                        e, k = SPLIT_W.index((layer, i)), tile[0]
                        at = (slots_before("D", layer, r, i) * PAIR + k) % D_RING
                        pe.wait_ge(tile_lo, slots_before("D", layer, m, i) * PAIR + (k + 1))
                        product(w_hi[:, e, k, :], d_hi[:, at, :], start)
                        product(w_lo[:, e, k, :], d_hi[:, at, :])
                        product(w_hi[:, e, k, :], d_lo[:, at, :], False, stop).then_inc(tile_used, 1)

            def mlp1(c):
                pe.wait_ge(z_loaded if c < CHUNKS - 1 else last_z_loaded, 32)
                for i in range(M1):
                    bank, cols = hid[i // NG][:, i % NG, :], slice(i * P, (i + 1) * P)
                    if c >= 1:
                        pe.wait_ge(h1_ready, M1 * c)
                    nc.tensor.matmul(bank, wt1_z[:, 0, cols], z_all[:, 0, c, :], start=True, stop=False)
                    nc.tensor.matmul(bank, wt1_z[:, 1, cols], z_all[:, 1, c, :], start=False, stop=False)
                    nc.tensor.matmul(bank, wt1_d[:, cols], dense_sb[:, c * COLS:(c + 1) * COLS],
                                     start=False, stop=True).then_inc(mlp1_done, 1)

            def mlp2(c):
                pe.wait_ge(h1_ready, M1 * (c + 1))
                if c >= 1:
                    pe.wait_ge(h2_ready, M2 * c)
                for i in range(M2):
                    for k in range(M1):
                        last = nc.tensor.matmul(acc[:, i, :], wt2_sb[:, k, i * P:(i + 1) * P], h1[:, c % 2, k, :],
                                                start=(k == 0), stop=(k == M1 - 1))
                    last.then_inc(mlp2_done, 1)

            def mlp3(c):
                pe.wait_ge(h2_ready, M2 * (c + 1))
                if c >= 1:
                    pe.wait_ge(y_ready, c)
                for k in range(M2):
                    last = nc.tensor.matmul(stage[0:1, :], wt3_sb[:, k:k + 1], h2[:, c % 2, k, :],
                                            start=(k == 0), stop=(k == M2 - 1))
                last.then_inc(mlp3_done, 1)

            pe.wait_ge(ident_ready, 1)
            transpose_block(0, 0, 0)
            transpose_block(1, 1, 0)
            pe.wait_ge(w0_summed, 1)
            contract(0, 0, 0)
            pe.wait_ge(w_parted, 1)

            def step(n, r, t):
                if r < BLOCKS - 2:
                    transpose_block(n + 2, r + 2, t if r % BPT < 2 else t + 1)
                if r < BLOCKS - 1:
                    contract(0, n + 1, r + 1)
                contract(1, n, r)
                if r >= 1:
                    contract(2, n - 1, r - 1)

            for r in range(BPT):
                step(r, r, 0)
            with pe.Fori(1, TILES - 1) as t:
                for j in range(BPT):
                    step(t * BPT + j, 2 * BPT + j, t)
            for r in range(BLOCKS - BPT, BLOCKS):
                step(r, r, TILES - 1)
            contract(2, BLOCKS - 1, BLOCKS - 1)
            pe.wait_ge(mlp_w_loaded, 16 * 7)
            pe.wait_ge(group_read, 3 * BLOCKS)
            mlp1(0)
            for c in range(CHUNKS):
                if c + 1 < CHUNKS:
                    mlp1(c + 1)
                mlp2(c)
                if c >= 1:
                    mlp3(c - 1)
            mlp3(CHUNKS - 1)


def kernel(**inputs):
    import concourse.bacc as bacc
    from concourse.bass_utils import run_bass_kernel_spmd

    nc = bacc.Bacc("TRN2", target_bir_lowering=False, num_devices=1)
    arrays = {}

    def given(name, a):
        a = np.ascontiguousarray(a)
        arrays[name] = a
        return nc.dram_tensor(name, a.shape, mybir.dt.from_np(a.dtype), kind="ExternalInput").ap()

    def arr(name):
        return np.asarray(inputs[name])

    ids = given("ids_in", arr("ids").reshape(TILES, P, FIELDS).transpose(1, 0, 2).reshape(P, TILES * FIELDS))
    tables = [given(f"tbl_{f}_in", arr(f"tbl_{f}")) for f in range(FIELDS)]
    dense_t = given("dense_t_in", arr("dense_ctx").T)

    w = arr("L0_rec_W0").reshape(FIELDS, FIELDS, LAYER)
    pairs = [np.zeros((FIELDS, DELTAS, K0, LAYER), w.dtype) for _ in range(2)]
    fields = np.arange(FIELDS)
    for k in range(K0):
        for j in range(DELTAS):
            delta = k * DELTAS + j
            if delta < OFFSETS:
                pairs[0][:, j, k] = w[fields, (fields + delta) % FIELDS]
                if delta > 0:
                    pairs[1][:, j, k] = w[(fields + delta) % FIELDS, fields]
    w0a = given("w0a_in", pairs[0].reshape(ROWS0, K0, LAYER))
    w0b = given("w0b_in", pairs[1].reshape(ROWS0, K0 * LAYER))

    def by_tile(w):
        full = np.zeros((KF * FQ, HIDDEN, LAYER), w.dtype)
        full[:FIELDS] = w.reshape(FIELDS, HIDDEN, LAYER)
        return full.reshape(KF, FQ, NG, GB, LAYER).transpose(1, 3, 2, 0, 4).reshape(P, NG * SG, PAIR * LAYER)

    w12 = np.stack([by_tile(arr("L0_rec_W1")), by_tile(arr("L0_rec_W2"))], axis=1)
    w_whole, w_split = (given(name, np.stack([w12[:, layer - 1, i] for layer, i in which], axis=1).reshape(P, -1))
                        for name, which in (("w_whole_in", WHOLE_W), ("w_split_in", SPLIT_W)))
    b_cin = given("b_cin_in", np.stack([arr(f"L0_rec_b{i}") for i in range(3)], axis=1))
    wt1 = given("wt1_in", arr("W_top1"))
    bt1 = given("bt1_in", arr("b_top1").reshape(M1, P).T)
    wt2 = given("wt2_in", arr("W_top2"))
    bt2 = given("bt2_in", arr("b_top2").reshape(M2, P).T)
    wt3 = given("wt3_in", arr("W_top3").reshape(M2, P).T)
    y = nc.dram_tensor("y_out", (1, BATCH), F32, kind="ExternalOutput").ap()

    build(nc, ids, tables, dense_t, w0a, w0b, w_whole, w_split, b_cin, wt1, bt1, wt2, bt2, wt3, y)
    result = run_bass_kernel_spmd(nc, [arrays], core_ids=[0])
    return result.results[0]["y_out"].reshape(BATCH, 1)
```
